# Optimizing a Trainium2 kernel written in Bass

```python
import numpy as np
import jax
import jax.numpy as jnp

def _softmax(x, axis=-1):
    return jax.nn.softmax(x, axis=axis)

def _gelu(x):
    return jax.nn.gelu(x, approximate=True)

def _silu(x):
    return jax.nn.silu(x)

def _sigmoid(x):
    return jax.nn.sigmoid(x)

def _layernorm(x, axis=-1, eps=1e-05):
    m = jnp.mean(x, axis=axis, keepdims=True)
    v = jnp.var(x, axis=axis, keepdims=True)
    return (x - m) / jnp.sqrt(v + eps)

def _scatter_add(tgt, idx, src, axis=0):
    return tgt.at[idx].add(src)

def _segment_sum(src, seg, n):
    return jax.ops.segment_sum(src, seg, n)
kernel_name = 'mk_recurrent_d1_jaxref_r8_82fbaa'

def setup_inputs(seed: int=0):
    np.random.seed(seed)
    _w = jnp.asarray

    def _L0_attn_setup():
        import jax, jax.numpy as jnp
        import numpy as np
        D_MODEL, D_STATE, HEAD_DIM, EXPAND, K, N_GROUPS = (128, 128, 64, 2, 4, 1)
        D_INNER = EXPAND * D_MODEL
        N_HEADS = D_INNER // HEAD_DIM
        D_PROJ = 2 * D_INNER + 2 * N_GROUPS * D_STATE + N_HEADS
        EPS = 1e-06

        def _silu(v):
            return v * jax.nn.sigmoid(v)
        key = jax.random.key(seed)
        ks = jax.random.split(key, 8)
        B, L = (2, 256)
        x = jax.random.normal(ks[0], (B, L, D_MODEL), dtype=jnp.float32)
        norm_w = jnp.ones((D_MODEL,), jnp.float32)
        in_proj_w = jax.random.normal(ks[1], (D_PROJ, D_MODEL), jnp.float32) * D_MODEL ** (-0.5)
        conv_w = jax.random.normal(ks[2], (D_INNER, 1, K), jnp.float32) * K ** (-0.5)
        conv_b = jnp.zeros((D_INNER,), jnp.float32)
        A_log = jnp.log(jax.random.uniform(ks[3], (N_HEADS,)) * 15.0 + 1.0)
        D = jnp.ones((N_HEADS,), jnp.float32)
        dt_bias = jnp.log(jax.random.uniform(ks[4], (N_HEADS,)) * 0.099 + 0.001)
        out_proj_w = jax.random.normal(ks[5], (D_MODEL, D_INNER), jnp.float32) * D_INNER ** (-0.5)
        return {'x': x, 'norm_w': norm_w, 'in_proj_w': in_proj_w, 'conv_w': conv_w, 'conv_b': conv_b, 'A_log': A_log, 'D': D, 'dt_bias': dt_bias, 'out_proj_w': out_proj_w}
    _L0_attn_in = _L0_attn_setup()

    def _L0_ffn_setup():
        import jax, jax.numpy as jnp
        import numpy as np
        D = 128
        H = 512
        E = 8
        B, N = (2, 256)
        key = jax.random.key(seed)
        ks = jax.random.split(key, 5)
        x = jax.random.normal(ks[0], (B, N, D), dtype=jnp.float32)
        W1 = jax.random.normal(ks[1], (E, D, H), dtype=jnp.float32) / np.sqrt(D)
        W2 = jax.random.normal(ks[2], (E, H, D), dtype=jnp.float32) / np.sqrt(H)
        Wg = jax.random.normal(ks[3], (D, E), dtype=jnp.float32) / np.sqrt(D)
        bg = jax.random.normal(ks[4], (E,), dtype=jnp.float32) * 0.01
        return {'x': x, 'W1': W1, 'W2': W2, 'Wg': Wg, 'bg': bg}
    _L0_ffn_in = _L0_ffn_setup()
    _d = {'L0_attn_x': _L0_attn_in['x'], 'L0_attn_norm_w': _L0_attn_in['norm_w'], 'L0_attn_in_proj_w': _L0_attn_in['in_proj_w'], 'L0_attn_conv_w': _L0_attn_in['conv_w'], 'L0_attn_conv_b': _L0_attn_in['conv_b'], 'L0_attn_A_log': _L0_attn_in['A_log'], 'L0_attn_D': _L0_attn_in['D'], 'L0_attn_dt_bias': _L0_attn_in['dt_bias'], 'L0_attn_out_proj_w': _L0_attn_in['out_proj_w'], 'L0_ffn_W1': _L0_ffn_in['W1'], 'L0_ffn_W2': _L0_ffn_in['W2'], 'L0_ffn_Wg': _L0_ffn_in['Wg'], 'L0_ffn_bg': _L0_ffn_in['bg']}
    _x0 = _d['L0_attn_x']
    _d['L0_attn_x'] = jax.random.normal(jax.random.fold_in(jax.random.key(seed), 1), (1, 2048, 128), dtype=_x0.dtype)
    del _x0
    return _d

def reference(L0_attn_x, L0_attn_norm_w, L0_attn_in_proj_w, L0_attn_conv_w, L0_attn_conv_b, L0_attn_A_log, L0_attn_D, L0_attn_dt_bias, L0_attn_out_proj_w, L0_ffn_W1, L0_ffn_W2, L0_ffn_Wg, L0_ffn_bg):

    def _L0_attn_ref(x, norm_w, in_proj_w, conv_w, conv_b, A_log, D, dt_bias, out_proj_w):
        import jax, jax.numpy as jnp
        import numpy as np
        D_MODEL, D_STATE, HEAD_DIM, EXPAND, K, N_GROUPS = (128, 128, 64, 2, 4, 1)
        D_INNER = EXPAND * D_MODEL
        N_HEADS = D_INNER // HEAD_DIM
        D_PROJ = 2 * D_INNER + 2 * N_GROUPS * D_STATE + N_HEADS
        EPS = 1e-06

        def _silu(v):
            return v * jax.nn.sigmoid(v)
        Bsz, L, _ = x.shape
        residual = x
        xn = x * jax.lax.rsqrt(jnp.mean(x * x, axis=-1, keepdims=True) + EPS) * norm_w
        proj = xn @ in_proj_w.T
        i = 0
        z = proj[..., i:i + D_INNER]
        i += D_INNER
        x_ssm = proj[..., i:i + D_INNER]
        i += D_INNER
        bc = N_GROUPS * D_STATE
        Bm = proj[..., i:i + bc].reshape(Bsz, L, N_GROUPS, D_STATE)
        i += bc
        Cm = proj[..., i:i + bc].reshape(Bsz, L, N_GROUPS, D_STATE)
        i += bc
        dt_raw = proj[..., i:i + N_HEADS]
        xc = jnp.transpose(x_ssm, (0, 2, 1))
        xc = jax.lax.conv_general_dilated(xc, conv_w, window_strides=(1,), padding=[(K - 1, 0)], dimension_numbers=('NCH', 'OIH', 'NCH'), feature_group_count=D_INNER)
        xc = xc + conv_b[None, :, None]
        x_conv = _silu(jnp.transpose(xc, (0, 2, 1)))
        dt = jax.nn.softplus(dt_raw + dt_bias)
        dA = jnp.exp(-jnp.exp(A_log)[None, None, :] * dt)
        x_heads = x_conv.reshape(Bsz, L, N_HEADS, HEAD_DIM)
        dt_x = dt[..., None] * x_heads
        group_idx = jnp.arange(N_HEADS) // (N_HEADS // N_GROUPS)
        Bg = Bm[:, :, group_idx, :]
        Cg = Cm[:, :, group_idx, :]

        def step(h, inp):
            dA_t, dtx_t, B_t, C_t = inp
            h = h * dA_t[..., None, None] + dtx_t[..., None] * B_t[:, :, None, :]
            y_t = jnp.einsum('bhpn,bhn->bhp', h, C_t)
            return (h, y_t)
        h0 = jnp.zeros((Bsz, N_HEADS, HEAD_DIM, D_STATE), jnp.float32)
        xs = (jnp.moveaxis(dA, 1, 0).astype(jnp.float32), jnp.moveaxis(dt_x, 1, 0).astype(jnp.float32), jnp.moveaxis(Bg, 1, 0).astype(jnp.float32), jnp.moveaxis(Cg, 1, 0).astype(jnp.float32))
        _, y = jax.lax.scan(step, h0, xs)
        y = jnp.moveaxis(y, 0, 1).astype(x.dtype)
        y = y + D[None, None, :, None] * x_heads
        y = y.reshape(Bsz, L, D_INNER) * _silu(z)
        return residual + y @ out_proj_w.T

    def _L0_ffn_ref(x, W1, W2, Wg, bg):
        import jax, jax.numpy as jnp
        import numpy as np
        D = 128
        H = 512
        E = 8
        B, N = (2, 256)
        b, n, d = x.shape
        e = Wg.shape[1]
        xf = x.reshape(b * n, d)
        logits = xf @ Wg + bg
        one_hot = jax.nn.one_hot(jnp.argmax(logits, axis=-1), e, dtype=x.dtype)
        h = jax.nn.gelu(jnp.einsum('td,edh->eth', xf, W1), approximate=True)
        y = jnp.einsum('eth,ehd->etd', h, W2)
        out = jnp.einsum('etd,te->td', y, one_hot)
        return out.reshape(b, n, d)
    x = L0_attn_x
    xn = _layernorm(x, axis=-1)
    s = _L0_attn_ref(xn, L0_attn_norm_w, L0_attn_in_proj_w, L0_attn_conv_w, L0_attn_conv_b, L0_attn_A_log, L0_attn_D, L0_attn_dt_bias, L0_attn_out_proj_w)
    g = _silu(_L0_ffn_ref(xn, L0_ffn_W1, L0_ffn_W2, L0_ffn_Wg, L0_ffn_bg))
    x = x + s * g
    return x

_drawn_inputs = setup_inputs


def setup_inputs(seed=0):
    import zlib

    import numpy as np

    out = dict(_drawn_inputs(seed))
    spreads = {'L0_attn_norm_w': (1.0, 0.2), 'L0_attn_conv_b': (0.0, 0.1), 'L0_attn_D': (1.0, 0.6)}
    factors = {}
    for name, (base, spread) in spreads.items():
        noise = np.random.default_rng([zlib.crc32(name.encode()), seed]).standard_normal(out[name].shape)
        drawn = base * np.exp(spread * noise) if base else spread * noise
        out[name] = jnp.asarray(drawn.astype(out[name].dtype))
    for name, factor in factors.items():
        out[name] = (out[name] * factor).astype(out[name].dtype)
    return out
```

```python
from contextlib import ExitStack

import concourse.bass as bass
from concourse import mybir

F32 = mybir.dt.float32
BF16 = mybir.dt.bfloat16
I32 = mybir.dt.int32
ALU = mybir.AluOpType
ACT = mybir.ActivationFunctionType
AX = mybir.AxisListType

P = 128
D = 128
NS = 128
DI = 256
NH = 4
HD = DI // NH
K = 4
E = 8
HID = 512
HC = HID // P
T = 2048
NT = T // P
NG = 4
GT = NT // NG
NJ = NT + E - 1
LN_EPS = 1e-5
RMS_EPS = 1e-6

WZ, WB, WC, WX, WDT, WG = 0, DI, DI + NS, DI + 2 * NS, 2 * DI + 2 * NS, 2 * DI + 2 * NS + NH
WCOLS = WG + E
NSM = NH + E

_AT = {}
_n = 0
for _name, _w in (("ident", P), ("upto", P), ("after", P), ("ones", P), ("iota", P), ("norm_w", 1), ("conv_b", 2),
                  ("conv_w", 2 * K), ("dt_bias", NH), ("A_log", NH), ("D", NH), ("bg", E), ("first", E),
                  ("steps", NT), ("tile_no", NT), ("row_no", 1), ("slot_tile", NJ), ("keep", NT * E)):
    _AT[_name] = (_n, _w)
    _n += _w
CCOLS = _n
S_DT, S_CUM, S_SUF, S_TOT, S_SLOT, SCOLS = 0, 4, 8, 12, 16, 17


def mamba_moe(nc, x, w_in, w_out, w1, w2, consts, out):
    with ExitStack() as ctx:
        def sb(name, shape, dt=F32):
            return ctx.enter_context(nc.sbuf_tensor(name, shape, dt))

        def sem(name):
            return ctx.enter_context(nc.semaphore(name))

        xn_rows = nc.dram_tensor("xn_rows", [T, D], F32, kind="Internal").ap()
        f_rows = nc.dram_tensor("f_rows", [NJ * P, D], F32, kind="Internal").ap()

        cst = sb("cst", [P, CCOLS])

        def c(name):
            at, w = _AT[name]
            return cst[:, at:at + w]

        w_raw = sb("w_raw", [P, WCOLS])
        w_s = sb("w_s", [P, WCOLS])
        wo = sb("wo", [P, 2, D])
        w2_s = sb("w2_s", [P, E * HC * D])
        xs = sb("xs", [P, NT, D])
        xn = sb("xn", [P, NT, D])
        xq = sb("xq", [P, NT, D])
        xqT = sb("xqT", [P, T])
        bn = sb("bn", [P, NT, 6])
        st = sb("st", [P, 12, NT])
        sm = sb("sm", [P, 12, NT * NH])
        neg_a = sb("neg_a", [P, NH])
        decay = sb("decay", [P, NT * NH])
        pack = sb("pack", [P, NT, SCOLS])
        L = sb("L", [P, NT * NH, P])
        r = sb("r", [P, 10, NT * E])
        hot = sb("hot", [P, NT, E], BF16)
        upto_before = sb("upto_before", [P, P], BF16)
        ones_bf = sb("ones_bf", [P, P], BF16)
        n_e = sb("n_e", [P, 8, E])
        tiles_cmp = sb("tiles_cmp", [P, E, NT])
        te_cmp = sb("te_cmp", [P, NJ, E])
        te_f = sb("te_f", [P, NJ])
        te = sb("te", [P, NJ], I32)
        slot_f = sb("slot_f", [P, NT])
        slot_i = sb("slot_i", [P, 3, NT], I32)
        slot_hl = sb("slot_hl", [P, 2, NT])
        hot_lo = sb("hot_lo", [P, NT, P], BF16)
        hot_hi = sb("hot_hi", [P, NT, NJ])
        tok_hi = sb("tok_hi", [P, NT, 2, NJ], BF16)
        tok_f = sb("tok_f", [P, 2, NJ])
        tok_i = sb("tok_i", [P, NJ], I32)
        xg = sb("xg", [P, 4, D])
        w1_t = sb("w1_t", [P, 4, HID])
        xgT = sb("xgT", [P, 4, P])
        hT = sb("hT", [P, 2, HC, P])
        f_t = sb("f_t", [P, 4, D])
        xqT_c = sb("xqT_c", [P, 2, P])
        x_c = sb("x_c", [P, 2, D])
        sc = sb("sc", [P, 2, SCOLS])
        x_raw = sb("x_raw", [P, 2, 2, P + K - 1])
        cv = sb("cv", [P, 2, 2, 2, P])
        cv_s = sb("cv_s", [P, 2, 2, P])
        bcT = sb("bcT", [P, 2, 2, P])
        b_tok = sb("b_tok", [P, 2, NS])
        z_s = sb("z_s", [P, 2, DI])
        x_v = sb("x_v", [P, 2, DI])
        g_m = sb("g_m", [P, 2, P])
        m = sb("m", [P, 2, NH, P])
        x_dt = sb("x_dt", [P, 2, DI])
        x_w = sb("x_w", [P, 2, DI])
        x_d = sb("x_d", [P, 2, DI])
        state = sb("state", [P, 2, DI])
        state_d = sb("state_d", [P, 2, DI])
        y = sb("y", [P, 4, DI])
        y_o = sb("y_o", [P, 2, DI])
        yT = sb("yT", [P, 2, 2, P])
        f_c = sb("f_c", [P, 2, D])
        g_c = sb("g_c", [P, 2, D])
        s_c = sb("s_c", [P, 2, D])
        sg_c = sb("sg_c", [P, 2, D])
        o_c = sb("o_c", [P, 2, D])

        bank = [ctx.enter_context(nc.psum_tensor(f"bank{i}", [P, 512], F32)) for i in range(8)]

        load_cst, load_w, load_wo, load_w2 = sem("load_cst"), sem("load_w"), sem("load_wo"), sem("load_w2")
        load_x = [sem(f"load_x{g}") for g in range(NG)]
        xn_stored = sem("xn_stored")
        dve_pre = sem("dve_pre")
        bn_done = sem("bn_done")
        std_done, rms_done = sem("std_done"), sem("rms_done")
        w_scaled = sem("w_scaled")
        xn_done, xq_done = sem("xn_done"), sem("xq_done")
        xqT_ps, xqT_done = sem("xqT_ps"), sem("xqT_done")
        small_ps = sem("small_ps")
        a_exp, abs_done, e_done, log_decay_done = sem("a_exp"), sem("abs_done"), sem("e_done"), sem("log_decay_done")
        cum_ps, cum_exp, pack_done = sem("cum_ps"), sem("cum_exp"), sem("pack_done")
        spread, seg_ps, L_done = sem("spread"), sem("seg_ps"), sem("L_done")
        bf_ready, hot_done, rank_ps, te_done, slot_done, inv_in, inv_ps, tok_done = (
            sem(n) for n in ("bf_ready", "hot_done", "rank_ps", "te_done", "slot_done", "inv_in", "inv_ps", "tok_done"))
        gathered = [sem(f"gathered{i}") for i in range(4)]
        w1_loaded = [sem(f"w1_loaded{i}") for i in range(4)]
        f_stored = [sem(f"f_stored{i}") for i in range(4)]
        xgT_ps, xgT_done, h_ps, h_done, f_ps, f_done = (
            sem(n) for n in ("xgT_ps", "xgT_done", "h_ps", "h_done", "f_ps", "f_done"))
        halo_zero, state_zero = sem("halo_zero"), sem("state_zero")
        xqT_in = [sem(f"xqT_in{b}") for b in range(2)]
        x_in = [sem(f"x_in{b}") for b in range(2)]
        sc_in = [sem(f"sc_in{b}") for b in range(2)]
        f_in = [sem(f"f_in{b}") for b in range(2)]
        out_stored = [sem(f"out_stored{b}") for b in range(2)]
        (x_ps, bcT_ps, zb_ps, y_ps, s_ps, yT_ps, o_ps, g_ps, xvT_ps) = (
            sem(n) for n in ("x_ps", "bcT_ps", "zb_ps", "y_ps", "s_ps", "yT_ps", "o_ps", "g_ps", "xvT_ps"))
        (bcT_done, z_done, b_done, cvs_done, xv_done, yT_done, gc_done) = (
            sem(n) for n in ("bcT_done", "z_done", "b_done", "cvs_done", "xv_done", "yT_done", "gc_done"))
        (raw_done, halo_done, tap, state_done, y_step, y_done, gm_done, m_done, s_done) = (
            sem(n) for n in ("raw_done", "halo_done", "tap", "state_done", "y_step", "y_done", "gm_done", "m_done",
                             "s_done"))
        (xdt_done, xw_done, xd_done, dec_done, sg_done, oc_done) = (
            sem(n) for n in ("xdt_done", "xw_done", "xd_done", "dec_done", "sg_done", "oc_done"))

        x_tiles = x[0].rearrange("(t p) d -> p t d", p=P)
        out_rows = out[0]

        def bc(ap, shape):
            return ap.to_broadcast(shape)

        block = ctx.enter_context(nc.Block())

        @block.sync
        def _(sp):
            for g in range(NG):
                sp.dma_start(xs[:, g * GT:(g + 1) * GT, :], x_tiles[:, g * GT:(g + 1) * GT, :]).then_inc(load_x[g], 16)
                if g == 0:
                    sp.dma_start(cst[:], consts).then_inc(load_cst, 16)
                if g == 1:
                    sp.dma_start(w_raw[:], w_in).then_inc(load_w, 16)
            sp.wait_ge(xn_done, NT)
            sp.dma_start(xn_rows.rearrange("(t p) d -> p t d", p=P), xn[:]).then_inc(xn_stored, 16)
            sp.dma_start(w2_s[:], w2).then_inc(load_w2, 16)
            sp.dma_start(wo[:].rearrange("p c d -> p (c d)"), w_out).then_inc(load_wo, 16)

            def load_w1(j, k):
                e = sp.value_load(te[0:1, bass.ds(j, 1)], min_val=0, max_val=E - 1)
                sp.dma_start(w1_t[:, k, :], w1[bass.ds(e, 1), :, :].rearrange("e p n -> p (e n)")).then_inc(w1_loaded[k], 16)

            def store_f(j, k):
                sp.wait_ge(f_done, j + 1)
                sp.dma_start(f_rows[bass.ds(j * P, P), :], f_t[:, k, :]).then_inc(f_stored[k], 16)

            sp.wait_ge(te_done, 1)
            for k in range(4):
                load_w1(k, k)
            with sp.Fori(0, (NJ - 3) // 4 - 1) as i:
                for k in range(4):
                    sp.wait_ge(h_ps, 4 * i + k + 1)
                    load_w1(4 * i + k + 4, k)
                    store_f(4 * i + k, k)
            last = NJ - 7
            for j in range(last, NJ):
                if j + 4 < NJ:
                    sp.wait_ge(h_ps, j + 1)
                    load_w1(j + 4, j % 4)
                store_f(j, j % 4)

            def load_xqT(n, b):
                sp.dma_start(xqT_c[:, b, :], xqT[:, bass.ds(n * P, P)]).then_inc(xqT_in[b], 16)

            def load_x_tile(n, b):
                sp.dma_start(x_c[:, b, :], xs[:, bass.ds(n, 1), :].rearrange("p a d -> p (a d)")).then_inc(x_in[b], 16)

            def load_scalars(n, b):
                sp.dma_start(sc[:, b, :], pack[:, bass.ds(n, 1), :].rearrange("p a d -> p (a d)")).then_inc(sc_in[b], 16)

            def store_out(n, b):
                sp.wait_ge(oc_done, n + 1)
                sp.dma_start(out_rows[bass.ds(n * P, P), :], o_c[:, b, :]).then_inc(out_stored[b], 16)

            sp.wait_ge(pack_done, 1)
            for n in range(2):
                load_xqT(n, n)
                load_scalars(n, n)
                load_x_tile(n, n)
            sp.wait_ge(zb_ps, 1)
            load_xqT(2, 0)

            def step(n, b, i):
                if not isinstance(n, int) or n + 3 < NT:
                    sp.wait_ge(zb_ps, n + 2)
                    load_xqT(n + 3, 1 - b)
                if not isinstance(n, int) or n >= 1:
                    store_out(n - 1, 1 - b)
                    if not isinstance(n, int) or n + 1 < NT:
                        load_x_tile(n + 1, 1 - b)
                if not isinstance(n, int) or n + 2 < NT:
                    sp.wait_ge(y_done, n + 1)
                    sp.wait_ge(dec_done, n + 1)
                    sp.wait_ge(f_in[b], 16 * (i + 1))
                    load_scalars(n + 2, b)

            step(0, 0, 0)
            step(1, 1, 0)
            with sp.Fori(1, NT // 2 - 2) as i:
                step(2 * i, 0, i)
                step(2 * i + 1, 1, i)
            for n in range(NT - 4, NT):
                step(n, n % 2, n // 2)
            store_out(NT - 1, 1)
            for b in range(2):
                sp.wait_ge(out_stored[b], 16 * NT // 2)

        @block.tensor
        def _(pe):
            mm, tr = nc.tensor.matmul, nc.tensor.transpose
            ident = c("ident")
            pe.wait_ge(load_cst, 16)
            for t in range(NT):
                pe.wait_ge(xq_done, t + 1)
                if t % GT == 0 and t // GT >= 2:
                    pe.wait_ge(xqT_done, t // GT - 1)
                ins = tr(bank[t // GT % 2][:, t % GT * P:(t % GT + 1) * P], xq[:, t, :], ident)
                if t % GT == GT - 1:
                    ins.then_inc(xqT_ps, 1)
            pe.wait_ge(w_scaled, 2)
            for t in range(NT):
                if t % GT == 0:
                    pe.wait_ge(xqT_done, t // GT + 1)
                ins = mm(bank[2][:, t * NSM:(t + 1) * NSM], xqT[:, t * P:(t + 1) * P], w_s[:, WDT:WDT + NSM],
                         start=True, stop=True)
            ins.then_inc(small_ps, 1)
            pe.wait_ge(log_decay_done, 1)
            for n, mask in enumerate(("upto", "after", "ones")):
                ins = mm(bank[3][:, n * NT * NH:(n + 1) * NT * NH], c(mask), decay[:], start=True, stop=True)
            ins.then_inc(cum_ps, 1)
            pe.wait_ge(xqT_done, NG)
            for n in range(2):
                pe.wait_ge(spread, n // 2 + 1)
                mm(bank[n][:], c("after"), L[:, n * NH:(n + 1) * NH, :], start=True, stop=True).then_inc(seg_ps, 1)
            with pe.Fori(1, NT // 2) as i:
                pe.wait_ge(spread, i + 1)
                for b in range(2):
                    pe.wait_ge(L_done, 2 * i + b - 1)
                    mm(bank[b][:], c("after"), L[:, bass.ds((2 * i + b) * NH, NH), :], start=True, stop=True)\
                        .then_inc(seg_ps, 1)
            pe.wait_ge(bf_ready, 2)
            pe.wait_ge(hot_done, 1)
            mm(bank[4][:, 0:NT * E], upto_before[:], hot[:].rearrange("p t e -> p (t e)"), start=True, stop=True)
            mm(bank[4][:, NT * E:2 * NT * E], ones_bf[:], hot[:].rearrange("p t e -> p (t e)"), start=True, stop=True)\
                .then_inc(rank_ps, 1)
            pe.wait_ge(inv_in, 1)
            for t in range(NT):
                ins = mm(bank[5][:, 0:2 * NJ], hot_lo[:, t, :], tok_hi[:, t, :, :].rearrange("p a j -> p (a j)"),
                         start=(t == 0), stop=(t == NT - 1))
            ins.then_inc(inv_ps, 1)

            def first_product(j, k):
                tr(bank[3][:, 0:P], xg[:, k, :], ident).then_inc(xgT_ps, 1)
                pe.wait_ge(xgT_done, j + 1)

            def products_in(j, k, i):
                pe.wait_ge(w1_loaded[k], 16 * (i + 1))
                for h in range(HC):
                    ins = mm(bank[k % 2][:, h * P:(h + 1) * P], w1_t[:, k, h * P:(h + 1) * P], xgT[:, k, :],
                             start=True, stop=True)
                ins.then_inc(h_ps, 1)

            def front(j, k, i, bank_free=True):
                pe.wait_ge(gathered[k], 16 * (i + 1))
                first_product(j, k)
                if bank_free:
                    pe.wait_ge(h_done, j - 1)
                products_in(j, k, i)

            def back(j, k, bank_free=True):
                e = pe.value_load(te[0:1, bass.ds(j, 1)], min_val=0, max_val=E - 1)
                pe.wait_ge(h_done, j + 1)
                if bank_free:
                    pe.wait_ge(f_done, j - 1)
                for h in range(HC):
                    ins = mm(bank[6 + k % 2][:, 0:D], hT[:, k % 2, h, :], w2_s[:, bass.ds(e * (HC * D) + h * D, D)],
                             start=(h == 0), stop=(h == HC - 1))
                ins.then_inc(f_ps, 1)

            pe.wait_ge(te_done, 1)
            pe.wait_ge(L_done, NT)
            pe.wait_ge(cum_exp, 1)
            pe.wait_ge(load_w2, 16)
            front(0, 0, 0, False)
            front(1, 1, 0, False)
            back(0, 0, False)
            front(2, 2, 0)
            back(1, 1, False)
            front(3, 3, 0)
            back(2, 2)
            front(4, 0, 1)
            back(3, 3)
            with pe.Fori(1, (NJ - 3) // 4) as i:
                for k in range(4):
                    j = 4 * i + k
                    front(j + 1, (k + 1) % 4, i + (k + 1) // 4)
                    back(j, k)
            for j in range(NJ - 3, NJ):
                if j + 1 < NJ:
                    front(j + 1, (j + 1) % 4, (j + 1) // 4)
                back(j, j % 4)

            def project(n, b, i, first=False):
                pe.wait_ge(xqT_in[b], 16 * (i + 1))
                if not first:
                    pe.wait_ge(raw_done, n)
                for h in range(2):
                    ins = mm(bank[0][:, h * P:(h + 1) * P], w_s[:, WX + h * P:WX + (h + 1) * P], xqT_c[:, b, :],
                             start=True, stop=True)
                ins.then_inc(x_ps, 1)
                if not first:
                    pe.wait_ge(bcT_done, n)
                for h in range(2):
                    ins = mm(bank[1][:, h * P:(h + 1) * P], w_s[:, WB + h * P:WB + (h + 1) * P], xqT_c[:, b, :],
                             start=True, stop=True)
                ins.then_inc(bcT_ps, 1)
                if not first:
                    pe.wait_ge(b_done, n)
                mm(bank[2][:, 0:DI + NS], xqT_c[:, b, :], w_s[:, WZ:WZ + DI + NS], start=True, stop=True)\
                    .then_inc(zb_ps, 1)

            def transpose_y(n, b, first=False):
                pe.wait_ge(y_done, n + 1)
                if not first:
                    pe.wait_ge(yT_done, n)
                for h in range(2):
                    ins = tr(bank[6][:, h * P:(h + 1) * P], y_o[:, b, h * P:(h + 1) * P], ident)
                ins.then_inc(yT_ps, 1)

            def products(n, b, first=False):
                pe.wait_ge(m_done, n + 1)
                pe.wait_ge(xdt_done, n + 1)
                if first:
                    pe.wait_ge(state_zero, 1)
                else:
                    pe.wait_ge(y_step, 3 * n)
                    pe.wait_ge(state_done, n)
                mm(bank[4][:, DI:2 * DI], bcT[:, b, 1, :], state[:, b, :], start=True, stop=True)
                for h in range(NH):
                    ins = mm(bank[4][:, h * HD:(h + 1) * HD], m[:, b, h, :], x_dt[:, b, h * HD:(h + 1) * HD],
                             start=True, stop=True)
                ins.then_inc(y_ps, 1)
                pe.wait_ge(xw_done, n + 1)
                pe.wait_ge(b_done, n + 1)
                mm(bank[5][:, 0:DI], b_tok[:, b, :], x_w[:, b, :], start=True, stop=True).then_inc(s_ps, 1)

            def project_out(n, b):
                pe.wait_ge(yT_done, n + 1)
                for h in range(2):
                    ins = mm(bank[7][:, 0:D], yT[:, b, h, :], wo[:, h, :], start=(h == 0), stop=(h == 1))
                ins.then_inc(o_ps, 1)

            def scores(n, b, first=False, second=False):
                pe.wait_ge(bcT_done, n + 1)
                mm(bank[7][:, D:2 * D], bcT[:, b, 0, :], bcT[:, b, 1, :], start=True, stop=True).then_inc(g_ps, 1)
                pe.wait_ge(cvs_done, n + 1)
                if not first:
                    pe.wait_ge(xv_done, n)
                for h in range(2):
                    ins = tr(bank[3][:, h * P:(h + 1) * P], cv_s[:, b, h, :], ident)
                ins.then_inc(xvT_ps, 1)

            def bank7_free(n, outputs):
                pe.wait_ge(gm_done, n + 1)
                if outputs:
                    pe.wait_ge(s_done, outputs)

            pe.wait_ge(f_ps, NJ)
            pe.wait_ge(f_done, NJ)
            pe.wait_ge(h_done, NJ)
            pe.wait_ge(load_wo, 16)
            project(0, 0, 0, True)
            scores(0, 0, True)
            project(1, 1, 0)
            products(0, 0, True)
            pe.wait_ge(gm_done, 1)
            scores(1, 1)

            def step(n, b, i_next, first=False):
                project(n + 1, 1 - b, i_next)
                transpose_y(n - 1, 1 - b, first)
                products(n, b)
                pe.wait_ge(gm_done, n + 1)
                if not first:
                    pe.wait_ge(s_done, n - 1)
                project_out(n - 1, 1 - b)
                scores(n + 1, 1 - b)

            step(1, 1, 1, True)
            with pe.Fori(1, NT // 2 - 1) as i:
                step(2 * i, 0, i)
                step(2 * i + 1, 1, i + 1)
            step(NT - 2, 0, NT // 2 - 1)
            n = NT - 1
            transpose_y(n - 1, 0)
            products(n, 1)
            pe.wait_ge(gm_done, n + 1)
            pe.wait_ge(s_done, n - 1)
            project_out(n - 1, 0)
            transpose_y(n, 1)
            pe.wait_ge(s_done, n)
            project_out(n, 1)

        @block.scalar
        def _(act):
            a = nc.scalar.activation
            act.wait_ge(dve_pre, 6)
            a(st[:, 5, :], st[:, 4, :], ACT.Sqrt).then_inc(std_done, 1)
            act.wait_ge(dve_pre, 10)
            a(st[:, 9, :], st[:, 8, :], ACT.Sqrt).then_inc(rms_done, 1)
            for g in range(NG):
                act.wait_ge(xqT_ps, g + 1)
                a(xqT[:, g * GT * P:(g + 1) * GT * P], bank[g % 2][:], ACT.Copy).then_inc(xqT_done, 1)
            act.wait_ge(load_cst, 16)
            a(neg_a[:], c("A_log"), ACT.Exp).then_inc(a_exp, 1)
            act.wait_ge(abs_done, 1)
            a(sm[:, 2, :], sm[:, 1, :], ACT.Exp, scale=-1.0).then_inc(e_done, 1)
            act.wait_ge(cum_ps, 1)
            a(sm[:, 8:11, :].rearrange("p a b -> p (a b)"), bank[3][:, 0:3 * NT * NH], ACT.Exp).then_inc(cum_exp, 1)
            with act.Fori(0, NT // 2) as i:
                for b in range(2):
                    act.wait_ge(seg_ps, 2 * i + b + 1)
                    a(L[:, bass.ds((2 * i + b) * NH, NH), :], bank[b][:].rearrange("p (h t) -> p h t", h=NH), ACT.Exp)\
                        .then_inc(L_done, 1)

            def hidden(j, k):
                act.wait_ge(h_ps, j + 1)
                a(hT[:, k, :, :], bank[k][:].rearrange("p (h t) -> p h t", h=HC), ACT.Gelu_apprx_tanh).then_inc(h_done, 1)

            hidden(0, 0)
            hidden(1, 1)
            with act.Fori(1, NJ // 2) as i:
                for k in range(2):
                    act.wait_ge(f_ps, 2 * i + k - 1)
                    hidden(2 * i + k, k)
            act.wait_ge(f_ps, NJ - 2)
            hidden(NJ - 1, 0)

            def early(n, b, wait=True):
                act.wait_ge(bcT_ps, n + 1)
                if wait:
                    act.wait_ge(y_ps, n - 1)
                    act.wait_ge(s_ps, n - 1)
                a(bcT[:, b, :, :], bank[1][:, 0:2 * P].rearrange("p (h t) -> p h t", h=2), ACT.Copy).then_inc(bcT_done, 1)

            def y_to_sbuf(n, b, wait=True):
                act.wait_ge(yT_ps, n + 1)
                if wait:
                    act.wait_ge(o_ps, n - 1)
                a(yT[:, b, :, :], bank[6][:, 0:2 * P].rearrange("p (h t) -> p h t", h=2), ACT.Copy).then_inc(yT_done, 1)

            def gates(n, b, wait=True):
                act.wait_ge(zb_ps, n + 1)
                if wait:
                    act.wait_ge(y_done, n - 1)
                a(z_s[:, b, :], bank[2][:, 0:DI], ACT.Silu).then_inc(z_done, 1)
                a(b_tok[:, b, :], bank[2][:, DI:DI + NS], ACT.Copy).then_inc(b_done, 1)

            def convolved(n, b, wait=True):
                act.wait_ge(tap, 8 * (n + 1))
                if wait:
                    act.wait_ge(xvT_ps, n - 1)
                a(cv_s[:, b, :, :], cv[:, b, 1, :, :], ACT.Silu).then_inc(cvs_done, 1)

            def inputs(n, b, wait=True):
                act.wait_ge(xvT_ps, n + 1)
                if wait:
                    act.wait_ge(xd_done, n - 1)
                a(x_v[:, b, :], bank[3][:, 0:DI], ACT.Copy).then_inc(xv_done, 1)

            def moe_gate(n, b, i, wait=True):
                act.wait_ge(f_in[b], 16 * (i + 1))
                if wait:
                    act.wait_ge(sg_done, n - 1)
                a(g_c[:, b, :], f_c[:, b, :], ACT.Silu).then_inc(gc_done, 1)

            for n in range(2):
                early(n, n, False)
                gates(n, n, False)
                convolved(n, n, False)
                inputs(n, n, False)

            def step(n, b, i, first=False):
                early(n + 1, 1 - b)
                y_to_sbuf(n - 1, 1 - b, not first)
                gates(n + 1, 1 - b)
                convolved(n + 1, 1 - b)
                moe_gate(n - 1, 1 - b, i, not first)
                inputs(n + 1, 1 - b)

            step(1, 1, 0, True)
            early(3, 1)
            y_to_sbuf(1, 1, False)
            gates(3, 1)
            convolved(3, 1)
            moe_gate(1, 1, 0, False)
            inputs(3, 1)
            step(3, 1, 1)
            with act.Fori(2, NT // 2 - 1) as i:
                step(2 * i, 0, i - 1)
                step(2 * i + 1, 1, i)
            step(NT - 2, 0, NT // 2 - 2)
            for n in (NT - 2, NT - 1):
                y_to_sbuf(n, n % 2)
                moe_gate(n, n % 2, n // 2)

        @block.gpsimd
        def _(pool):
            g = nc.gpsimd
            g.memset(x_raw[:, 1, :, P:P + K - 1], 0.0).then_inc(halo_zero, 1)
            g.memset(state[:, 0, :], 0.0).then_inc(state_zero, 1)
            pool.wait_ge(load_cst, 16)
            g.tensor_copy(ones_bf[:], c("ones")).then_inc(bf_ready, 1)
            pool.wait_ge(log_decay_done, 1)
            for n in range(NT // 2):
                src = decay[:, 2 * NH * n:2 * NH * (n + 1)].unsqueeze(2)
                g.affine_select(out=L[:, 2 * NH * n:2 * NH * (n + 1), :], in_=bc(src, [P, 2 * NH, P]),
                                pattern=[[0, 2 * NH], [1, P]], base=0, channel_multiplier=-1,
                                compare_op=ALU.is_ge, fill=0.0).then_inc(spread, 1)
            pool.wait_ge(tok_done, 1)
            pool.wait_ge(xn_stored, 16)
            for j in range(NJ):
                if j >= 4:
                    pool.wait_ge(xgT_ps, j - 3)
                g.indirect_dma_start(xg[:, j % 4, :], None, xn_rows, bass.IndirectOffsetOnAxis(tok_i[:, j:j + 1], 0))\
                    .then_inc(gathered[j % 4], 16)

            def heads(ap):
                return ap.rearrange("p (h d) -> p h d", h=NH)

            def per_head(b, at):
                return bc(sc[:, b, at:at + NH].unsqueeze(2), [P, NH, HD])

            def scaled_inputs(n, b, i, wait=True):
                pool.wait_ge(xv_done, n + 1)
                pool.wait_ge(sc_in[b], 16 * (i + 1))
                if wait:
                    pool.wait_ge(gc_done, n - 1)
                    pool.wait_ge(y_ps, n - 1)
                g.tensor_tensor(heads(x_dt[:, b, :]), heads(x_v[:, b, :]), per_head(b, S_DT), ALU.mult).then_inc(xdt_done, 1)
                g.indirect_dma_start(f_c[:, b, :], None, f_rows,
                                     bass.IndirectOffsetOnAxis(sc[:, b, S_SLOT:S_SLOT + 1].bitcast(I32), 0))\
                    .then_inc(f_in[b], 16)
                if wait:
                    pool.wait_ge(s_ps, n - 1)
                g.tensor_tensor(heads(x_w[:, b, :]), heads(x_v[:, b, :]), per_head(b, S_SUF), ALU.mult).then_inc(xw_done, 1)
                if wait:
                    pool.wait_ge(y_done, n - 1)
                g.tensor_tensor(heads(x_d[:, b, :]), heads(x_v[:, b, :]), bc(c("D").unsqueeze(2), [P, NH, HD]),
                                ALU.mult).then_inc(xd_done, 1)

            def decayed_state(n, b, i, first=False):
                pool.wait_ge(sc_in[b], 16 * (i + 1))
                if first:
                    pool.wait_ge(state_zero, 1)
                else:
                    pool.wait_ge(state_done, n)
                g.tensor_tensor(heads(state_d[:, b, :]), heads(state[:, b, :]), per_head(b, S_TOT), ALU.mult)\
                    .then_inc(dec_done, 1)

            def finish(n, b, i, wait=True):
                pool.wait_ge(gc_done, n + 1)
                pool.wait_ge(s_done, n + 1)
                g.tensor_tensor(sg_c[:, b, :], s_c[:, b, :], g_c[:, b, :], ALU.mult).then_inc(sg_done, 1)
                pool.wait_ge(sg_done, n + 1)
                pool.wait_ge(x_in[b], 16 * (i + 1))
                if wait:
                    pool.wait_ge(out_stored[b], 16 * i)
                g.tensor_tensor(o_c[:, b, :], sg_c[:, b, :], x_c[:, b, :], ALU.add).then_inc(oc_done, 1)

            for k in range(4):
                pool.wait_ge(f_stored[k], 16 * ((NJ - k + 3) // 4))
            scaled_inputs(0, 0, 0, False)
            decayed_state(0, 0, 0, True)
            scaled_inputs(1, 1, 0, False)

            def step(n, b, i, i_next, i_prev, first=False):
                decayed_state(n, b, i)
                finish(n - 1, 1 - b, i_prev, not first)
                scaled_inputs(n + 1, 1 - b, i_next)

            step(1, 1, 0, 1, 0, True)
            decayed_state(2, 0, 1)
            finish(1, 1, 0, False)
            scaled_inputs(3, 1, 1)
            step(3, 1, 1, 2, 1)
            with pool.Fori(2, NT // 2 - 1) as i:
                step(2 * i, 0, i, i, i - 1)
                step(2 * i + 1, 1, i, i + 1, i)
            step(NT - 2, 0, NT // 2 - 1, NT // 2 - 1, NT // 2 - 2)
            decayed_state(NT - 1, 1, NT // 2 - 1)
            for n in (NT - 2, NT - 1):
                finish(n, n % 2, n // 2)

        @block.vector
        def _(dve):
            v = nc.vector
            count = [0]

            def then(ins):
                count[0] += 1
                ins.then_inc(dve_pre, 1)
                dve.wait_ge(dve_pre, count[0])

            for g in range(NG):
                dve.wait_ge(load_x[g], 16)
                for t in range(g * GT, (g + 1) * GT):
                    v.bn_stats(bn[:, t, :], xs[:, t, :]).then_inc(bn_done, 1)
            dve.wait_ge(bn_done, NT)

            def col(k):
                return bn[:, :, k]

            s_ = [st[:, k, :] for k in range(12)]
            v.tensor_tensor(s_[0], col(1), col(4), ALU.add).then_inc(dve_pre, 1)
            v.tensor_tensor(s_[1], col(1), col(4), ALU.subtract).then_inc(dve_pre, 1)
            count[0] = 2
            then(v.tensor_tensor(s_[2], col(2), col(5), ALU.add))
            then(v.scalar_tensor_tensor(out=s_[3], in0=s_[1], scalar=0.25, in1=s_[1], op0=ALU.mult, op1=ALU.mult))
            then(v.scalar_tensor_tensor(out=s_[3], in0=s_[2], scalar=1.0 / D, in1=s_[3], op0=ALU.mult, op1=ALU.add))
            then(v.tensor_scalar(s_[4], s_[3], LN_EPS, None, ALU.add))
            dve.wait_ge(std_done, 1)
            then(v.reciprocal(s_[6], s_[5]))
            then(v.tensor_tensor(s_[7], s_[6], s_[6], ALU.mult))
            then(v.tensor_tensor(s_[7], s_[7], s_[3], ALU.mult))
            then(v.tensor_scalar(s_[8], s_[7], RMS_EPS, None, ALU.add))
            then(v.tensor_scalar(s_[0], s_[0], 0.5, None, ALU.mult))
            dve.wait_ge(rms_done, 1)
            then(v.reciprocal(s_[10], s_[9]))
            then(v.tensor_tensor(s_[11], s_[6], s_[10], ALU.mult))
            with dve.Fori(0, NG) as i:
                for k in range(GT):
                    t = GT * i + k
                    at = bass.ds(t, 1)
                    v.tensor_scalar(xq[:, at, :], xs[:, at, :], st[:, 0, at], st[:, 11, at], ALU.subtract, ALU.mult)\
                        .then_inc(xq_done, 1)
                    v.tensor_scalar(xn[:, at, :], xs[:, at, :], st[:, 0, at], st[:, 6, at], ALU.subtract, ALU.mult)\
                        .then_inc(xn_done, 1)
            dve.wait_ge(load_cst, 16)
            dve.wait_ge(load_w, 16)
            v.tensor_scalar(w_s[:, 0:WG], w_raw[:, 0:WG], c("norm_w"), None, ALU.mult).then_inc(w_scaled, 1)
            v.tensor_copy(w_s[:, WG:WG + E], w_raw[:, WG:WG + E]).then_inc(w_scaled, 1)
            v.tensor_tensor(upto_before[:], c("upto"), c("ident"), ALU.subtract).then_inc(bf_ready, 1)

            dve.wait_ge(small_ps, 1)
            small = bank[2][:, 0:NT * NSM].rearrange("p (t k) -> p t k", k=NSM)
            q = [sm[:, k, :] for k in range(12)]
            q3 = [sm[:, k, :].rearrange("p (t h) -> p t h", h=NH) for k in range(12)]
            then(v.tensor_tensor(q3[0], small[:, :, 0:NH], bc(c("dt_bias").unsqueeze(1), [P, NT, NH]), ALU.add))
            v.scalar_tensor_tensor(out=q[1], in0=q[0], scalar=-1.0, in1=q[0], op0=ALU.mult, op1=ALU.max).then_inc(abs_done, 1)
            R = [r[:, k, :].rearrange("p (t e) -> p t e", e=E) for k in range(10)]
            then(v.tensor_tensor(R[0], small[:, :, NH:NSM], bc(st[:, 9, :].unsqueeze(2), [P, NT, E]), ALU.mult))
            then(v.tensor_tensor(R[1], R[0], bc(c("bg").unsqueeze(1), [P, NT, E]), ALU.add))
            dve.wait_ge(e_done, 1)
            then(v.tensor_scalar(q[3], q[2], 2.0, None, ALU.add))
            then(v.reciprocal(q[4], q[3]))
            then(v.tensor_tensor(q[4], q[4], q[2], ALU.mult))
            then(v.tensor_tensor(q[5], q[4], q[4], ALU.mult))
            then(v.tensor_scalar(q[6], q[5], 1.0 / 17, None, ALU.mult))
            for k in (15, 13, 11, 9, 7, 5, 3):
                then(v.scalar_tensor_tensor(out=q[6], in0=q[6], scalar=1.0 / k, in1=q[5], op0=ALU.add, op1=ALU.mult))
            then(v.scalar_tensor_tensor(out=q[6], in0=q[6], scalar=1.0, in1=q[4], op0=ALU.add, op1=ALU.mult))
            then(v.tensor_scalar(q[7], q[0], 0.0, 0.5, ALU.max, ALU.mult))
            then(v.tensor_tensor(q[7], q[7], q[6], ALU.add))
            dt = pack[:, :, S_DT:S_DT + NH]
            then(v.tensor_scalar(dt, q3[7], 2.0, None, ALU.mult))
            dve.wait_ge(a_exp, 1)
            v.scalar_tensor_tensor(out=decay[:].rearrange("p (t h) -> p t h", h=NH), in0=dt, scalar=-1.0,
                                   in1=bc(neg_a[:].unsqueeze(1), [P, NT, NH]), op0=ALU.mult, op1=ALU.mult)\
                .then_inc(log_decay_done, 1)

            then(v.tensor_reduce(r[:, 2, 0:NT], R[1], AX.X, ALU.max))
            then(v.tensor_tensor(R[3], R[1], bc(r[:, 2, 0:NT].unsqueeze(2), [P, NT, E]), ALU.is_equal))
            first = bc(c("first").unsqueeze(1), [P, NT, E])
            then(v.tensor_tensor(R[3], R[3], first, ALU.mult))
            then(v.tensor_reduce(r[:, 2, 0:NT], R[3], AX.X, ALU.max))
            v.tensor_tensor(hot[:], first, bc(r[:, 2, 0:NT].unsqueeze(2), [P, NT, E]), ALU.is_equal).then_inc(hot_done, 1)
            dve.wait_ge(cum_exp, 1)
            v.tensor_copy(pack[:, :, S_CUM:S_CUM + NH], q3[8])
            v.tensor_tensor(pack[:, :, S_SUF:S_SUF + NH], q3[9], dt, ALU.mult)
            then(v.tensor_copy(pack[:, :, S_TOT:S_TOT + NH], q3[10]))
            dve.wait_ge(rank_ps, 1)
            by_e = [r[:, k, :].rearrange("p (e t) -> p e t", e=E) for k in range(10)]
            then(v.tensor_copy(by_e[4], bank[4][:, NT * E:2 * NT * E].rearrange("p (t e) -> p e t", e=E)))
            then(v.tensor_tensor_scan(r[:, 5, :], c("keep"), r[:, 4, :], 0.0, ALU.mult, ALU.add))
            then(v.tensor_tensor(r[:, 6, :], r[:, 5, :], r[:, 4, :], ALU.subtract))
            total = by_e[5][:, :, NT - 1:NT]
            then(v.tensor_tensor(tiles_cmp[:], bc(total, [P, E, NT]), bc(c("steps").unsqueeze(1), [P, E, NT]), ALU.is_gt))
            then(v.tensor_reduce(n_e[:, 0, :], tiles_cmp[:], AX.X, ALU.add))
            then(v.tensor_tensor_scan(n_e[:, 1, :], c("ones")[:, 0:E], n_e[:, 0, :], 0.0, ALU.mult, ALU.add))
            then(v.tensor_tensor(n_e[:, 2, :], n_e[:, 1, :], n_e[:, 0, :], ALU.subtract))
            then(v.tensor_tensor(te_cmp[:], bc(n_e[:, 1, :].unsqueeze(1), [P, NJ, E]),
                                 bc(c("slot_tile").unsqueeze(2), [P, NJ, E]), ALU.is_le))
            then(v.tensor_reduce(te_f[:], te_cmp[:], AX.X, ALU.add))
            v.tensor_scalar(te[:], te_f[:], float(E - 1), None, ALU.min).then_inc(te_done, 1)
            then(v.tensor_tensor(R[7], bank[4][:, 0:NT * E].rearrange("p (t e) -> p t e", e=E),
                                 by_e[6].rearrange("p e t -> p t e"), ALU.add))
            then(v.scalar_tensor_tensor(out=R[7], in0=bc(n_e[:, 2, :].unsqueeze(1), [P, NT, E]), scalar=float(P),
                                        in1=R[7], op0=ALU.mult, op1=ALU.add))
            then(v.tensor_tensor(R[7], R[7], hot[:], ALU.mult))
            then(v.tensor_reduce(slot_f[:], R[7], AX.X, ALU.add))
            then(v.tensor_copy(slot_i[:, 0, :], slot_f[:]))
            then(v.tensor_scalar(slot_i[:, 1, :], slot_i[:, 0, :], 7, None, ALU.logical_shift_right))
            then(v.tensor_scalar(slot_i[:, 2, :], slot_i[:, 0, :], P - 1, None, ALU.bitwise_and))
            then(v.tensor_copy(slot_hl[:], slot_i[:, 1:3, :]))
            v.tensor_copy(pack[:, :, S_SLOT:S_SLOT + 1].bitcast(I32), slot_i[:, 0, :].unsqueeze(2)).then_inc(pack_done, 1)
            v.tensor_tensor(hot_lo[:], bc(c("iota").unsqueeze(1), [P, NT, P]), bc(slot_hl[:, 1, :].unsqueeze(2), [P, NT, P]),
                            ALU.is_equal)
            then(v.tensor_tensor(hot_hi[:], bc(c("slot_tile").unsqueeze(1), [P, NT, NJ]),
                                 bc(slot_hl[:, 0, :].unsqueeze(2), [P, NT, NJ]), ALU.is_equal))
            then(v.tensor_tensor(tok_hi[:, :, 0, :], hot_hi[:], bc(c("tile_no").unsqueeze(2), [P, NT, NJ]), ALU.mult))
            v.tensor_scalar(tok_hi[:, :, 1, :], hot_hi[:], c("row_no"), None, ALU.mult).then_inc(inv_in, 1)
            dve.wait_ge(inv_ps, 1)
            then(v.tensor_copy(tok_f[:].rearrange("p a j -> p (a j)"), bank[5][:, 0:2 * NJ]))
            v.scalar_tensor_tensor(out=tok_i[:], in0=tok_f[:, 0, :], scalar=float(P), in1=tok_f[:, 1, :],
                                   op0=ALU.mult, op1=ALU.add).then_inc(tok_done, 1)

            def gathered_tile(j, k):
                dve.wait_ge(xgT_ps, j + 1)
                v.tensor_copy(xgT[:, k, :], bank[3][:, 0:P]).then_inc(xgT_done, 1)

            def output_tile(j, k, i=None):
                dve.wait_ge(f_ps, j + 1)
                if i is not None:
                    dve.wait_ge(f_stored[k], 16 * i)
                v.tensor_copy(f_t[:, k, :], bank[6 + k % 2][:, 0:D]).then_inc(f_done, 1)

            for j in range(4):
                gathered_tile(j, j)
                if j >= 1:
                    output_tile(j - 1, j - 1)
            gathered_tile(4, 0)
            output_tile(3, 3)
            with dve.Fori(1, (NJ - 3) // 4) as i:
                for k in range(4):
                    gathered_tile(4 * i + k + 1, (k + 1) % 4)
                    output_tile(4 * i + k, k, i)
            for j in range(NJ - 3, NJ):
                if j + 1 < NJ:
                    gathered_tile(j + 1, (j + 1) % 4)
                output_tile(j, j % 4, j // 4)

            def convolve(n, b, first=False):
                dve.wait_ge(x_ps, n + 1)
                v.tensor_copy(x_raw[:, b, :, K - 1:], bank[0][:, 0:2 * P].rearrange("p (h t) -> p h t", h=2))\
                    .then_inc(raw_done, 1)
                if first:
                    dve.wait_ge(halo_zero, 1)
                v.tensor_copy(x_raw[:, b, :, 0:K - 1], x_raw[:, 1 - b, :, P:P + K - 1]).then_inc(halo_done, 1)
                dve.wait_ge(raw_done, n + 1)
                cw = c("conv_w")
                for h in range(2):
                    v.tensor_scalar(cv[:, b, 0, h, :], x_raw[:, b, h, K - 1:K - 1 + P], cw[:, h * K + K - 1:h * K + K],
                                    c("conv_b")[:, h:h + 1], ALU.mult, ALU.add).then_inc(tap, 1)
                dve.wait_ge(halo_done, n + 1)
                for k in range(K - 1):
                    for h in range(2):
                        dve.wait_ge(tap, 8 * n + 2 * k + h + 1)
                        v.scalar_tensor_tensor(out=cv[:, b, (k + 1) % 2, h, :], in0=x_raw[:, b, h, k:k + P],
                                               scalar=cw[:, h * K + k:h * K + k + 1], in1=cv[:, b, k % 2, h, :],
                                               op0=ALU.mult, op1=ALU.add).then_inc(tap, 1)

            def next_state(n, b):
                dve.wait_ge(s_ps, n + 1)
                dve.wait_ge(dec_done, n + 1)
                v.tensor_tensor(state[:, 1 - b, :], state_d[:, b, :], bank[5][:, 0:DI], ALU.add).then_inc(state_done, 1)

            def heads(ap):
                return ap.rearrange("p (h d) -> p h d", h=NH)

            def gated_output(n, b, i, first=False):
                dve.wait_ge(sc_in[b], 16 * (i + 1))
                dve.wait_ge(y_ps, n + 1)
                v.tensor_tensor(heads(y[:, 0, :]), heads(bank[4][:, DI:2 * DI]),
                                bc(sc[:, b, S_CUM:S_CUM + NH].unsqueeze(2), [P, NH, HD]), ALU.mult).then_inc(y_step, 1)
                dve.wait_ge(xd_done, n + 1)
                v.tensor_tensor(y[:, 1, :], bank[4][:, 0:DI], x_d[:, b, :], ALU.add).then_inc(y_step, 1)
                dve.wait_ge(y_step, 3 * n + 2)
                v.tensor_tensor(y[:, 2, :], y[:, 0, :], y[:, 1, :], ALU.add).then_inc(y_step, 1)
                dve.wait_ge(y_step, 3 * n + 3)
                dve.wait_ge(z_done, n + 1)
                v.tensor_tensor(y_o[:, b, :], y[:, 2, :], z_s[:, b, :], ALU.mult).then_inc(y_done, 1)

            def decayed_scores(n, b):
                dve.wait_ge(g_ps, n + 1)
                v.tensor_tensor(g_m[:, b, :], bank[7][:, D:2 * D], c("upto"), ALU.mult).then_inc(gm_done, 1)
                dve.wait_ge(gm_done, n + 1)
                v.tensor_tensor(m[:, b, :, :], L[:, bass.ds(n * NH, NH), :], bc(g_m[:, b, :].unsqueeze(1), [P, NH, P]),
                                ALU.mult).then_inc(m_done, 1)

            def block_output(n, b):
                dve.wait_ge(o_ps, n + 1)
                v.tensor_tensor(s_c[:, b, :], bank[7][:, 0:D], xn[:, bass.ds(n, 1), :].rearrange("p a d -> p (a d)"),
                                ALU.add).then_inc(s_done, 1)

            dve.wait_ge(L_done, NT)
            convolve(0, 0, True)
            decayed_scores(0, 0)
            convolve(1, 1)
            next_state(0, 0)
            gated_output(0, 0, 0)
            decayed_scores(1, 1)

            def step(n, b, i, convolve_next=True, wait=True):
                if convolve_next:
                    if wait:
                        dve.wait_ge(cvs_done, n)
                    convolve(n + 1, 1 - b)
                    next_state(n, b)
                dve.wait_ge(yT_ps, n - 1) if wait else None
                gated_output(n, b, i)
                if convolve_next:
                    decayed_scores(n + 1, 1 - b)
                if wait:
                    dve.wait_ge(sg_done, n - 2) if wait != "short" else None
                block_output(n - 1, 1 - b)

            step(1, 1, 0, wait=False)
            step(2, 0, 1, wait="short")
            step(3, 1, 1)
            with dve.Fori(2, NT // 2 - 1) as i:
                step(2 * i, 0, i)
                step(2 * i + 1, 1, i)
            step(NT - 2, 0, NT // 2 - 1)
            step(NT - 1, 1, NT // 2 - 1, convolve_next=False)
            dve.wait_ge(sg_done, NT - 2)
            block_output(NT - 1, 1)


def _lay_out(np, a):
    k = np.arange(P)
    part = {
        "ident": np.eye(P), "upto": k[:, None] <= k[None, :], "after": k[:, None] > k[None, :],
        "ones": np.ones((P, P)), "iota": np.broadcast_to(k, (P, P)),
        "first": np.broadcast_to(E - np.arange(E), (P, E)), "steps": np.broadcast_to(P * np.arange(NT), (P, NT)),
        "tile_no": np.broadcast_to(np.arange(NT), (P, NT)), "row_no": k[:, None],
        "slot_tile": np.broadcast_to(np.arange(NJ), (P, NJ)),
        "keep": np.broadcast_to(np.arange(NT * E) % NT != 0, (P, NT * E)),
    }
    part = {n: p.astype(np.float32) for n, p in part.items()}
    part["norm_w"] = a["L0_attn_norm_w"][:, None]
    part["conv_b"] = a["L0_attn_conv_b"].reshape(2, P).T
    part["conv_w"] = a["L0_attn_conv_w"].reshape(2, P, K).transpose(1, 0, 2).reshape(P, 2 * K)
    for name, key in (("dt_bias", "L0_attn_dt_bias"), ("A_log", "L0_attn_A_log"), ("D", "L0_attn_D"), ("bg", "L0_ffn_bg")):
        part[name] = np.broadcast_to(a[key], (P, a[key].shape[0]))
    return np.concatenate([part[n] for n in _AT], axis=1)


def kernel(**inputs):
    import numpy as np
    import concourse.bacc as bacc
    from concourse.bass_utils import run_bass_kernel_spmd

    a = {k: np.asarray(v) for k, v in inputs.items()}
    w = a["L0_attn_in_proj_w"].T
    z, xx, bb, cc, dt = (w[:, 0:DI], w[:, DI:2 * DI], w[:, 2 * DI:2 * DI + NS], w[:, 2 * DI + NS:2 * DI + 2 * NS],
                         w[:, 2 * DI + 2 * NS:])
    arrays = {
        "x": a["L0_attn_x"],
        "w_in": np.concatenate([z, bb, cc, xx, dt, a["L0_ffn_Wg"]], axis=1),
        "w_out": a["L0_attn_out_proj_w"].T.reshape(2, P, D).transpose(1, 0, 2).reshape(P, 2 * D),
        "w1": a["L0_ffn_W1"],
        "w2": a["L0_ffn_W2"].reshape(E, HC, P, D).transpose(2, 0, 1, 3).reshape(P, E * HC * D),
        "consts": _lay_out(np, a),
    }
    arrays = {k: np.ascontiguousarray(v) for k, v in arrays.items()}
    nc = bacc.Bacc("TRN2", target_bir_lowering=False, num_devices=1)
    aps = {k: nc.dram_tensor(k, v.shape, mybir.dt.from_np(v.dtype), kind="ExternalInput").ap() for k, v in arrays.items()}
    out = nc.dram_tensor("out", (1, T, D), F32, kind="ExternalOutput").ap()
    mamba_moe(nc, **aps, out=out)
    return run_bass_kernel_spmd(nc, [arrays], core_ids=[0]).results[0]["out"]
```

```python
from contextlib import ExitStack

import concourse.bass as bass
from concourse import mybir

F32 = mybir.dt.float32
BF16 = mybir.dt.bfloat16
I32 = mybir.dt.int32
ALU = mybir.AluOpType
ACT = mybir.ActivationFunctionType
AX = mybir.AxisListType

P = 128
D = 128
NS = 128
DI = 256
NH = 4
HD = DI // NH
K = 4
E = 8
HID = 512
HC = HID // P
T = 2048
NT = T // P
NG = 4
GT = NT // NG
GP = GT * P
NJ = NT + E - 1
SPLIT = 6
LN_EPS = 1e-5
RMS_EPS = 1e-6

WZ, WB, WC, WX, WDT, WG = 0, DI, DI + NS, DI + 2 * NS, 2 * DI + 2 * NS, 2 * DI + 2 * NS + NH
WCOLS = WG + E
NSM = NH + E

_AT = {}
_n = 0
for _name, _w in (("ident", P), ("upto", P), ("after", P), ("ones", P), ("iota", P), ("norm_w", 1), ("conv_b", 2),
                  ("conv_w", 2 * K), ("dt_bias", NH), ("A_log", NH), ("D", NH), ("bg", E), ("first", E),
                  ("steps", NT), ("tile_no", NT), ("row_no", 1), ("slot_tile", NJ), ("keep", NT * E)):
    _AT[_name] = (_n, _w)
    _n += _w
CCOLS = _n
S_DT, S_CUM, S_SUF, S_TOT, S_SLOT, SCOLS = 0, 4, 8, 12, 16, 17


def mamba_moe(nc, x, w_in, w_out, w1, w2, consts, out):
    with ExitStack() as ctx:
        def sb(name, shape, dt=F32):
            return ctx.enter_context(nc.sbuf_tensor(name, shape, dt))

        def sem(name):
            return ctx.enter_context(nc.semaphore(name))

        xn_rows = nc.dram_tensor("xn_rows", [T, D], F32, kind="Internal").ap()
        f_rows = nc.dram_tensor("f_rows", [NJ * P, D], F32, kind="Internal").ap()

        cst = sb("cst", [P, CCOLS])

        def c(name):
            at, w = _AT[name]
            return cst[:, at:at + w]

        w_raw = sb("w_raw", [P, WCOLS])
        w_s = sb("w_s", [P, WCOLS])
        wo = sb("wo", [P, 2, D])
        w2_s = sb("w2_s", [P, E * HC * D])
        xs = sb("xs", [P, NT, D])
        xn = sb("xn", [P, NT, D])
        xqT = sb("xqT", [P, T])
        bn = sb("bn", [P, NT, 6])
        st = sb("st", [P, 12, NT])
        sm = sb("sm", [P, 12, NT * NH])
        neg_a = sb("neg_a", [P, NH])
        decay = sb("decay", [P, NT * NH])
        pack = sb("pack", [P, NT, SCOLS])
        L = sb("L", [P, NT * NH, P])
        r = sb("r", [P, 10, NT * E])
        hot = sb("hot", [P, NT, E], BF16)
        upto_before = sb("upto_before", [P, P], BF16)
        ones_bf = sb("ones_bf", [P, P], BF16)
        n_e = sb("n_e", [P, 8, E])
        tiles_cmp = sb("tiles_cmp", [P, E, NT])
        te_cmp = sb("te_cmp", [P, NJ, E])
        te_f = sb("te_f", [P, NJ])
        te = sb("te", [P, NJ], I32)
        slot_f = sb("slot_f", [P, NT])
        slot_i = sb("slot_i", [P, 3, NT], I32)
        slot_hl = sb("slot_hl", [P, 2, NT])
        hot_lo = sb("hot_lo", [P, NT, P], BF16)
        hot_hi = sb("hot_hi", [P, NT, NJ])
        tok_hi = sb("tok_hi", [P, NT, 2, NJ], BF16)
        tok_f = sb("tok_f", [P, 2, NJ])
        tok_i = sb("tok_i", [P, NJ], I32)
        xg = sb("xg", [P, 4, D])
        w1_t = sb("w1_t", [P, 4, HID])
        xgT = sb("xgT", [P, 4, P])
        hT = sb("hT", [P, 2, HC, P])
        f_t = sb("f_t", [P, 4, D])
        xqT_c = sb("xqT_c", [P, 2, P])
        x_c = sb("x_c", [P, 2, D])
        sc = sb("sc", [P, 2, SCOLS])
        x_raw = sb("x_raw", [P, 2, T + K - 1])
        cv_acc = sb("cv_acc", [P, 2, 2, GP])
        cv = sb("cv", [P, 2, T])
        xq = cv[:, 0, :].rearrange("p (t d) -> p t d", d=D)
        cv_s = sb("cv_s", [P, 2, 2, P])
        bcT = sb("bcT", [P, 2, 2, P])
        b_tok = sb("b_tok", [P, 2, NS])
        z_s = sb("z_s", [P, 2, DI])
        x_v = sb("x_v", [P, 2, DI])
        g_m = sb("g_m", [P, 2, P])
        m = sb("m", [P, 2, NH, P])
        x_dt = sb("x_dt", [P, 2, DI])
        x_w = sb("x_w", [P, 2, DI])
        x_d = sb("x_d", [P, 2, DI])
        state = sb("state", [P, 2, DI])
        state_d = sb("state_d", [P, 2, DI])
        y = sb("y", [P, 4, DI])
        y_o = sb("y_o", [P, 2, DI])
        yT = sb("yT", [P, 2, 2, P])
        f_c = sb("f_c", [P, 2, D])
        g_c = sb("g_c", [P, 2, D])
        s_c = sb("s_c", [P, 2, D])
        sg_c = sb("sg_c", [P, 2, D])
        o_c = sb("o_c", [P, 2, D])

        bank = [ctx.enter_context(nc.psum_tensor(f"bank{i}", [P, 512], F32)) for i in range(8)]

        load_cst, load_w, load_wo, load_w2 = sem("load_cst"), sem("load_w"), sem("load_wo"), sem("load_w2")
        load_x = [sem(f"load_x{g}") for g in range(NG)]
        xn_stored = sem("xn_stored")
        dve_pre = sem("dve_pre")
        bn_done = sem("bn_done")
        std_done, rms_done = sem("std_done"), sem("rms_done")
        w_scaled = sem("w_scaled")
        x_centred, xn_done, xq_done = sem("x_centred"), sem("xn_done"), sem("xq_done")
        xqT_ps, xqT_done = sem("xqT_ps"), sem("xqT_done")
        small_ps = sem("small_ps")
        a_exp, abs_done, e_done, log_decay_done = sem("a_exp"), sem("abs_done"), sem("e_done"), sem("log_decay_done")
        cum_ps, cum_exp, pack_done = sem("cum_ps"), sem("cum_exp"), sem("pack_done")
        spread, seg_ps, L_done = sem("spread"), sem("seg_ps"), sem("L_done")
        bf_ready, hot_done, rank_ps, te_done, slot_done, inv_in, inv_ps, tok_done = (
            sem(n) for n in ("bf_ready", "hot_done", "rank_ps", "te_done", "slot_done", "inv_in", "inv_ps", "tok_done"))
        gathered = [sem(f"gathered{i}") for i in range(4)]
        w1_loaded = [sem(f"w1_loaded{i}") for i in range(4)]
        f_stored = [sem(f"f_stored{i}") for i in range(4)]
        xgT_ps, xgT_done, h_ps, h_done, f_ps, f_done = (
            sem(n) for n in ("xgT_ps", "xgT_done", "h_ps", "h_done", "f_ps", "f_done"))
        halo_zero, state_zero = sem("halo_zero"), sem("state_zero")
        xqT_in = [sem(f"xqT_in{b}") for b in range(2)]
        x_in = [sem(f"x_in{b}") for b in range(2)]
        sc_in = [sem(f"sc_in{b}") for b in range(2)]
        f_in = [sem(f"f_in{b}") for b in range(2)]
        out_stored = [sem(f"out_stored{b}") for b in range(2)]
        (x_ps, bcT_ps, zb_ps, y_ps, s_ps, yT_ps, o_ps, g_ps, xvT_ps) = (
            sem(n) for n in ("x_ps", "bcT_ps", "zb_ps", "y_ps", "s_ps", "yT_ps", "o_ps", "g_ps", "xvT_ps"))
        (bcT_done, z_done, b_done, cvs_done, xv_done, yT_done, gc_done) = (
            sem(n) for n in ("bcT_done", "z_done", "b_done", "cvs_done", "xv_done", "yT_done", "gc_done"))
        (raw_done, halo_done, tap, state_done, y_step, y_done, gm_done, m_done, s_done) = (
            sem(n) for n in ("raw_done", "halo_done", "tap", "state_done", "y_step", "y_done", "gm_done", "m_done",
                             "s_done"))
        (xdt_done, xw_done, xd_done, dec_done, sg_done, oc_done) = (
            sem(n) for n in ("xdt_done", "xw_done", "xd_done", "dec_done", "sg_done", "oc_done"))

        x_tiles = x[0].rearrange("(t p) d -> p t d", p=P)
        out_rows = out[0]

        def bc(ap, shape):
            return ap.to_broadcast(shape)

        block = ctx.enter_context(nc.Block())

        @block.sync
        def _(sp):
            for g in range(NG):
                sp.dma_start(xs[:, g * GT:(g + 1) * GT, :], x_tiles[:, g * GT:(g + 1) * GT, :]).then_inc(load_x[g], 16)
                if g == 0:
                    sp.dma_start(cst[:], consts).then_inc(load_cst, 16)
                if g == 1:
                    sp.dma_start(w_raw[:], w_in).then_inc(load_w, 16)
            sp.wait_ge(xn_done, NG)
            sp.dma_start(xn_rows.rearrange("(t p) d -> p t d", p=P), xn[:]).then_inc(xn_stored, 16)
            sp.dma_start(w2_s[:], w2).then_inc(load_w2, 16)
            sp.dma_start(wo[:].rearrange("p c d -> p (c d)"), w_out).then_inc(load_wo, 16)

            def load_w1(j, k):
                e = sp.value_load(te[0:1, bass.ds(j, 1)], min_val=0, max_val=E - 1)
                sp.dma_start(w1_t[:, k, :], w1[bass.ds(e, 1), :, :].rearrange("e p n -> p (e n)")).then_inc(w1_loaded[k], 16)

            def store_f(j, k):
                sp.wait_ge(f_done, j + 1)
                sp.dma_start(f_rows[bass.ds(j * P, P), :], f_t[:, k, :]).then_inc(f_stored[k], 16)

            sp.wait_ge(te_done, 1)
            for k in range(4):
                load_w1(k, k)
            with sp.Fori(0, (NJ - 3) // 4 - 1) as i:
                for k in range(4):
                    sp.wait_ge(h_ps, 4 * i + k + 1)
                    load_w1(4 * i + k + 4, k)
                    store_f(4 * i + k, k)
            last = NJ - 7
            for j in range(last, NJ):
                if j + 4 < NJ:
                    sp.wait_ge(h_ps, j + 1)
                    load_w1(j + 4, j % 4)
                store_f(j, j % 4)

            def load_xqT(n, b):
                sp.dma_start(xqT_c[:, b, :], xqT[:, bass.ds(n * P, P)]).then_inc(xqT_in[b], 16)

            def load_x_tile(n, b):
                sp.dma_start(x_c[:, b, :], xs[:, bass.ds(n, 1), :].rearrange("p a d -> p (a d)")).then_inc(x_in[b], 16)

            def load_scalars(n, b):
                sp.dma_start(sc[:, b, :], pack[:, bass.ds(n, 1), :].rearrange("p a d -> p (a d)")).then_inc(sc_in[b], 16)

            def store_out(n, b):
                sp.wait_ge(oc_done, n + 1)
                sp.dma_start(out_rows[bass.ds(n * P, P), :], o_c[:, b, :]).then_inc(out_stored[b], 16)

            sp.wait_ge(pack_done, 1)
            for n in range(2):
                load_xqT(n, n)
                load_scalars(n, n)
                load_x_tile(n, n)
            sp.wait_ge(zb_ps, 1)
            load_xqT(2, 0)

            def step(n, b, i):
                if not isinstance(n, int) or n + 3 < NT:
                    sp.wait_ge(zb_ps, n + 2)
                    load_xqT(n + 3, 1 - b)
                if not isinstance(n, int) or n + 2 < NT:
                    sp.wait_ge(xw_done, n + 1)
                    sp.wait_ge(f_in[b], 16 * (i + 1))
                    load_scalars(n + 2, b)
                if not isinstance(n, int) or n >= 1:
                    store_out(n - 1, 1 - b)
                    if not isinstance(n, int) or n + 1 < NT:
                        load_x_tile(n + 1, 1 - b)

            step(0, 0, 0)
            step(1, 1, 0)
            with sp.Fori(1, NT // 2 - 2) as i:
                step(2 * i, 0, i)
                step(2 * i + 1, 1, i)
            for n in range(NT - 4, NT):
                step(n, n % 2, n // 2)
            store_out(NT - 1, 1)
            for b in range(2):
                sp.wait_ge(out_stored[b], 16 * NT // 2)

        @block.tensor
        def _(pe):
            mm, tr = nc.tensor.matmul, nc.tensor.transpose
            ident = c("ident")
            pe.wait_ge(load_cst, 16)
            def transpose_group(g):
                if g >= 2:
                    pe.wait_ge(xqT_done, g - 1)
                for t in range(g * GT, (g + 1) * GT):
                    pe.wait_ge(xq_done, t + 1)
                    ins = tr(bank[g % 2][:, t % GT * P:(t % GT + 1) * P], xq[:, t, :], ident)
                ins.then_inc(xqT_ps, 1)

            def small_products(g):
                pe.wait_ge(xqT_done, g + 1)
                for t in range(g * GT, (g + 1) * GT):
                    ins = mm(bank[2][:, t * NSM:(t + 1) * NSM], xqT[:, t * P:(t + 1) * P], w_s[:, WDT:WDT + NSM],
                             start=True, stop=True)
                return ins

            transpose_group(0)
            pe.wait_ge(w_scaled, 2)
            for g in range(1, NG):
                transpose_group(g)
                small_products(g - 1)
            small_products(NG - 1).then_inc(small_ps, 1)
            pe.wait_ge(log_decay_done, 1)
            for n, mask in enumerate(("upto", "after", "ones")):
                ins = mm(bank[3][:, n * NT * NH:(n + 1) * NT * NH], c(mask), decay[:], start=True, stop=True)
            ins.then_inc(cum_ps, 1)
            pe.wait_ge(bf_ready, 2)
            pe.wait_ge(hot_done, 1)
            mm(bank[4][:, 0:NT * E], upto_before[:], hot[:].rearrange("p t e -> p (t e)"), start=True, stop=True)
            mm(bank[4][:, NT * E:2 * NT * E], ones_bf[:], hot[:].rearrange("p t e -> p (t e)"), start=True, stop=True)\
                .then_inc(rank_ps, 1)
            pe.wait_ge(xqT_done, NG)

            def log_decays(n, b, wait=True):
                if wait:
                    pe.wait_ge(L_done, n - 1)
                mm(bank[b][:], c("after"), L[:, bass.ds(n * NH, NH), :], start=True, stop=True).then_inc(seg_ps, 1)

            for n in range(2):
                pe.wait_ge(spread, 1)
                log_decays(n, n, False)
            with pe.Fori(1, SPLIT) as i:
                pe.wait_ge(spread, i + 1)
                for b in range(2):
                    log_decays(2 * i + b, b)
            pe.wait_ge(inv_in, 1)
            for t in range(NT):
                ins = mm(bank[5][:, 0:2 * NJ], hot_lo[:, t, :], tok_hi[:, t, :, :].rearrange("p a j -> p (a j)"),
                         start=(t == 0), stop=(t == NT - 1))
            ins.then_inc(inv_ps, 1)
            with pe.Fori(SPLIT, NT // 2) as i:
                pe.wait_ge(spread, i + 1)
                for b in range(2):
                    log_decays(2 * i + b, b)

            def transpose_in(j, k, i, bank_free=True):
                pe.wait_ge(gathered[k], 16 * (i + 1))
                if bank_free:
                    pe.wait_ge(xgT_done, j)
                tr(bank[3][:, 0:P], xg[:, k, :], ident).then_inc(xgT_ps, 1)

            def hidden(j, k, i, bank_free=True):
                pe.wait_ge(w1_loaded[k], 16 * (i + 1))
                pe.wait_ge(xgT_done, j + 1)
                if bank_free:
                    pe.wait_ge(h_done, j - 1)
                for h in range(HC):
                    ins = mm(bank[k % 2][:, h * P:(h + 1) * P], w1_t[:, k, h * P:(h + 1) * P], xgT[:, k, :],
                             start=True, stop=True)
                ins.then_inc(h_ps, 1)

            def back(j, k, bank_free=True):
                e = pe.value_load(te[0:1, bass.ds(j, 1)], min_val=0, max_val=E - 1)
                pe.wait_ge(h_done, j + 1)
                if bank_free:
                    pe.wait_ge(f_done, j - 1)
                for h in range(HC):
                    ins = mm(bank[6 + k % 2][:, 0:D], hT[:, k % 2, h, :], w2_s[:, bass.ds(e * (HC * D) + h * D, D)],
                             start=(h == 0), stop=(h == HC - 1))
                ins.then_inc(f_ps, 1)

            def tile(j, k, i):
                if not isinstance(j, int) or j + 2 < NJ:
                    transpose_in(j + 2, (k + 2) % 4, i + (k + 2) // 4)
                if not isinstance(j, int) or j + 1 < NJ:
                    hidden(j + 1, (k + 1) % 4, i + (k + 1) // 4, not isinstance(j, int) or j >= 1)
                back(j, k, not isinstance(j, int) or j >= 2)

            def conv_channels(i, h):
                mm(bank[4 + h][:], w_s[:, WX + h * P:WX + (h + 1) * P], xqT[:, bass.ds((i - 1) * GP, GP)],
                   start=True, stop=True).then_inc(x_ps, 1)

            pe.wait_ge(te_done, 1)
            pe.wait_ge(L_done, NT)
            pe.wait_ge(cum_exp, 1)
            transpose_in(0, 0, 0, False)
            transpose_in(1, 1, 0)
            hidden(0, 0, 0, False)
            pe.wait_ge(load_w2, 16)
            for j in range(4):
                tile(j, j, 0)
            pe.wait_ge(tok_done, 1)
            with pe.Fori(1, NG + 1) as i:
                for k in range(4):
                    if k < 2:
                        conv_channels(i, k)
                    tile(4 * i + k, k, i)
            for j in range(4 * (NG + 1), NJ):
                tile(j, j % 4, j // 4)

            def project(n, b, i, first=False):
                pe.wait_ge(xqT_in[b], 16 * (i + 1))
                if not first:
                    pe.wait_ge(bcT_done, n)
                for h in range(2):
                    ins = mm(bank[1][:, h * P:(h + 1) * P], w_s[:, WB + h * P:WB + (h + 1) * P], xqT_c[:, b, :],
                             start=True, stop=True)
                ins.then_inc(bcT_ps, 1)
                if not first:
                    pe.wait_ge(b_done, n)
                mm(bank[2][:, 0:DI + NS], xqT_c[:, b, :], w_s[:, WZ:WZ + DI + NS], start=True, stop=True)\
                    .then_inc(zb_ps, 1)

            def transpose_y(n, b, first=False):
                pe.wait_ge(y_done, n + 1)
                if not first:
                    pe.wait_ge(yT_done, n)
                for h in range(2):
                    ins = tr(bank[6][:, h * P:(h + 1) * P], y_o[:, b, h * P:(h + 1) * P], ident)
                ins.then_inc(yT_ps, 1)

            def products(n, b, first=False):
                pe.wait_ge(m_done, n + 1)
                pe.wait_ge(xdt_done, n + 1)
                if first:
                    pe.wait_ge(state_zero, 1)
                else:
                    pe.wait_ge(y_step, 3 * n)
                    pe.wait_ge(state_done, n)
                mm(bank[4][:, DI:2 * DI], bcT[:, b, 1, :], state[:, b, :], start=True, stop=True)
                for h in range(NH):
                    ins = mm(bank[4][:, h * HD:(h + 1) * HD], m[:, b, h, :], x_dt[:, b, h * HD:(h + 1) * HD],
                             start=True, stop=True)
                ins.then_inc(y_ps, 1)
                pe.wait_ge(xw_done, n + 1)
                pe.wait_ge(b_done, n + 1)
                mm(bank[5][:, 0:DI], b_tok[:, b, :], x_w[:, b, :], start=True, stop=True).then_inc(s_ps, 1)

            def project_out(n, b, first=False):
                pe.wait_ge(yT_done, n + 1)
                if not first:
                    pe.wait_ge(s_done, n)
                for h in range(2):
                    ins = mm(bank[7][:, 0:D], yT[:, b, h, :], wo[:, h, :], start=(h == 0), stop=(h == 1))
                ins.then_inc(o_ps, 1)

            def scores(n, b, first=False):
                pe.wait_ge(bcT_done, n + 1)
                if not first:
                    pe.wait_ge(gm_done, n)
                mm(bank[0][:, 0:P], bcT[:, b, 0, :], bcT[:, b, 1, :], start=True, stop=True).then_inc(g_ps, 1)

            def transpose_inputs(n, b, first=False):
                pe.wait_ge(cvs_done, n + 1)
                if not first:
                    pe.wait_ge(xv_done, n)
                for h in range(2):
                    ins = tr(bank[3][:, h * P:(h + 1) * P], cv_s[:, b, h, :], ident)
                ins.then_inc(xvT_ps, 1)

            pe.wait_ge(f_done, NJ)
            pe.wait_ge(h_done, NJ)
            pe.wait_ge(load_wo, 16)
            project(0, 0, 0, True)
            transpose_inputs(0, 0, True)
            scores(0, 0, True)

            def step(n, b, i_next):
                if not isinstance(n, int) or n + 1 < NT:
                    transpose_inputs(n + 1, 1 - b)
                    project(n + 1, 1 - b, i_next)
                if not isinstance(n, int) or n >= 1:
                    transpose_y(n - 1, 1 - b, isinstance(n, int) and n == 1)
                if not isinstance(n, int) or n + 1 < NT:
                    scores(n + 1, 1 - b)
                products(n, b, isinstance(n, int) and n == 0)
                if not isinstance(n, int) or n >= 1:
                    project_out(n - 1, 1 - b, isinstance(n, int) and n == 1)

            step(0, 0, 0)
            step(1, 1, 1)
            with pe.Fori(1, NT // 2 - 1) as i:
                step(2 * i, 0, i)
                step(2 * i + 1, 1, i + 1)
            step(NT - 2, 0, NT // 2 - 1)
            step(NT - 1, 1, None)
            transpose_y(NT - 1, 1)
            project_out(NT - 1, 1)

        @block.scalar
        def _(act):
            a = nc.scalar.activation
            act.wait_ge(dve_pre, 6)
            a(st[:, 5, :], st[:, 4, :], ACT.Sqrt).then_inc(std_done, 1)
            act.wait_ge(dve_pre, 10)
            a(st[:, 9, :], st[:, 8, :], ACT.Sqrt).then_inc(rms_done, 1)
            for g in range(NG):
                act.wait_ge(xqT_ps, g + 1)
                a(xqT[:, g * GT * P:(g + 1) * GT * P], bank[g % 2][:], ACT.Copy).then_inc(xqT_done, 1)
            act.wait_ge(load_cst, 16)
            a(neg_a[:], c("A_log"), ACT.Exp).then_inc(a_exp, 1)
            act.wait_ge(abs_done, 1)
            a(sm[:, 2, :], sm[:, 1, :], ACT.Exp, scale=-1.0).then_inc(e_done, 1)
            act.wait_ge(cum_ps, 1)
            a(sm[:, 8:11, :].rearrange("p a b -> p (a b)"), bank[3][:, 0:3 * NT * NH], ACT.Exp).then_inc(cum_exp, 1)
            with act.Fori(0, NT // 2) as i:
                for b in range(2):
                    act.wait_ge(seg_ps, 2 * i + b + 1)
                    a(L[:, bass.ds((2 * i + b) * NH, NH), :], bank[b][:].rearrange("p (h t) -> p h t", h=NH), ACT.Exp)\
                        .then_inc(L_done, 1)

            def hidden(j, k):
                act.wait_ge(h_ps, j + 1)
                a(hT[:, k, :, :], bank[k][:].rearrange("p (h t) -> p h t", h=HC), ACT.Gelu_apprx_tanh).then_inc(h_done, 1)

            hidden(0, 0)
            hidden(1, 1)
            for j in (2, 3):
                act.wait_ge(f_ps, j - 1)
                hidden(j, j % 2)
            with act.Fori(1, NG + 1) as i:
                for k in range(4):
                    act.wait_ge(f_ps, 4 * i + k - 1)
                    hidden(4 * i + k, k % 2)
                    if k < 2:
                        act.wait_ge(x_ps, 2 * i + k - 1)
                        a(x_raw[:, k, bass.ds((i - 1) * GP + K - 1, GP)], bank[4 + k][:], ACT.Copy).then_inc(raw_done, 1)
            for j in range(4 * (NG + 1), NJ):
                act.wait_ge(f_ps, j - 1)
                hidden(j, j % 2)

            def early(n, b, wait=True):
                act.wait_ge(bcT_ps, n + 1)
                if wait:
                    act.wait_ge(y_ps, n - 1)
                    act.wait_ge(s_ps, n - 1)
                a(bcT[:, b, :, :], bank[1][:, 0:2 * P].rearrange("p (h t) -> p h t", h=2), ACT.Copy).then_inc(bcT_done, 1)

            def y_to_sbuf(n, b, wait=True):
                act.wait_ge(yT_ps, n + 1)
                if wait:
                    act.wait_ge(o_ps, n - 1)
                a(yT[:, b, :, :], bank[6][:, 0:2 * P].rearrange("p (h t) -> p h t", h=2), ACT.Copy).then_inc(yT_done, 1)

            def gates(n, b, wait=True):
                act.wait_ge(zb_ps, n + 1)
                if wait:
                    act.wait_ge(y_done, n - 1)
                a(z_s[:, b, :], bank[2][:, 0:DI], ACT.Silu).then_inc(z_done, 1)
                a(b_tok[:, b, :], bank[2][:, DI:DI + NS], ACT.Copy).then_inc(b_done, 1)

            def convolved(n, b, wait=True):
                if wait:
                    act.wait_ge(xvT_ps, n - 1)
                a(cv_s[:, b, :, :], cv[:, :, bass.ds(n * P, P)], ACT.Silu).then_inc(cvs_done, 1)

            def inputs(n, b, wait=True):
                act.wait_ge(xvT_ps, n + 1)
                if wait:
                    act.wait_ge(xd_done, n - 1)
                a(x_v[:, b, :], bank[3][:, 0:DI], ACT.Copy).then_inc(xv_done, 1)

            def moe_gate(n, b, i, wait=True):
                act.wait_ge(f_in[b], 16 * (i + 1))
                if wait:
                    act.wait_ge(sg_done, n - 1)
                a(g_c[:, b, :], f_c[:, b, :], ACT.Silu).then_inc(gc_done, 1)

            act.wait_ge(tap, 2 * K * NG)
            convolved(0, 0, False)
            early(0, 0, False)
            inputs(0, 0, False)
            gates(0, 0, False)
            convolved(1, 1, False)

            def step(n, b, i_prev):
                known = isinstance(n, int)
                if not known or n + 1 < NT:
                    inputs(n + 1, 1 - b, not known or n >= 1)
                    early(n + 1, 1 - b, not known or n >= 1)
                    gates(n + 1, 1 - b, not known or n >= 1)
                if not known or n + 2 < NT:
                    convolved(n + 2, b)
                if not known or n >= 1:
                    y_to_sbuf(n - 1, 1 - b, not known or n >= 3)
                    moe_gate(n - 1, 1 - b, i_prev, not known or n >= 3)

            for n in range(4):
                step(n, n % 2, (n - 1) // 2)
            with act.Fori(2, NT // 2 - 1) as i:
                step(2 * i, 0, i - 1)
                step(2 * i + 1, 1, i)
            step(NT - 2, 0, NT // 2 - 2)
            step(NT - 1, 1, NT // 2 - 1)
            y_to_sbuf(NT - 1, 1)
            moe_gate(NT - 1, 1, NT // 2 - 1)

        @block.gpsimd
        def _(pool):
            g = nc.gpsimd
            g.memset(x_raw[:, :, 0:K - 1], 0.0).then_inc(halo_zero, 1)
            g.memset(state[:, 0, :], 0.0).then_inc(state_zero, 1)
            pool.wait_ge(load_cst, 16)
            g.tensor_copy(ones_bf[:], c("ones")).then_inc(bf_ready, 1)
            for n in range(NG):
                if n == 0:
                    pool.wait_ge(dve_pre, 11)
                at = slice(n * GT, (n + 1) * GT)
                g.tensor_tensor(xn[:, at, :], xs[:, at, :], bc(st[:, 0, at].unsqueeze(2), [P, GT, D]), ALU.subtract)\
                    .then_inc(x_centred, 1)
                pool.wait_ge(x_centred, n + 1)
                g.tensor_tensor(xn[:, at, :], xn[:, at, :], bc(st[:, 6, at].unsqueeze(2), [P, GT, D]), ALU.mult)\
                    .then_inc(xn_done, 1)
            pool.wait_ge(log_decay_done, 1)
            for n in range(NT // 2):
                src = decay[:, 2 * NH * n:2 * NH * (n + 1)].unsqueeze(2)
                g.affine_select(out=L[:, 2 * NH * n:2 * NH * (n + 1), :], in_=bc(src, [P, 2 * NH, P]),
                                pattern=[[0, 2 * NH], [1, P]], base=0, channel_multiplier=-1,
                                compare_op=ALU.is_ge, fill=0.0).then_inc(spread, 1)
            pool.wait_ge(tok_done, 1)
            pool.wait_ge(xn_stored, 16)
            for j in range(NJ):
                if j >= 4:
                    pool.wait_ge(xgT_ps, j - 3)
                g.indirect_dma_start(xg[:, j % 4, :], None, xn_rows, bass.IndirectOffsetOnAxis(tok_i[:, j:j + 1], 0))\
                    .then_inc(gathered[j % 4], 16)

            def heads(ap):
                return ap.rearrange("p (h d) -> p h d", h=NH)

            def per_head(b, at):
                return bc(sc[:, b, at:at + NH].unsqueeze(2), [P, NH, HD])

            def scaled_inputs(n, b, i, wait=True):
                pool.wait_ge(xv_done, n + 1)
                pool.wait_ge(sc_in[b], 16 * (i + 1))
                if wait:
                    pool.wait_ge(gc_done, n - 1)
                    pool.wait_ge(y_ps, n - 1)
                g.tensor_tensor(heads(x_dt[:, b, :]), heads(x_v[:, b, :]), per_head(b, S_DT), ALU.mult).then_inc(xdt_done, 1)
                g.indirect_dma_start(f_c[:, b, :], None, f_rows,
                                     bass.IndirectOffsetOnAxis(sc[:, b, S_SLOT:S_SLOT + 1].bitcast(I32), 0))\
                    .then_inc(f_in[b], 16)
                if wait:
                    pool.wait_ge(s_ps, n - 1)
                g.tensor_tensor(heads(x_w[:, b, :]), heads(x_v[:, b, :]), per_head(b, S_SUF), ALU.mult).then_inc(xw_done, 1)
                if wait:
                    pool.wait_ge(y_done, n - 1)
                g.tensor_tensor(heads(x_d[:, b, :]), heads(x_v[:, b, :]), bc(c("D").unsqueeze(2), [P, NH, HD]),
                                ALU.mult).then_inc(xd_done, 1)

            def finish(n, b, i, wait=True):
                pool.wait_ge(x_in[b], 16 * (i + 1))
                if wait:
                    pool.wait_ge(out_stored[b], 16 * i)
                pool.wait_ge(sg_done, n + 1)
                g.tensor_tensor(o_c[:, b, :], sg_c[:, b, :], x_c[:, b, :], ALU.add).then_inc(oc_done, 1)

            for k in range(4):
                pool.wait_ge(f_stored[k], 16 * ((NJ - k + 3) // 4))
            scaled_inputs(0, 0, 0, False)
            scaled_inputs(1, 1, 0, False)

            def step(n, b, i, i_prev):
                known = isinstance(n, int)
                if not known or n + 1 < NT:
                    scaled_inputs(n + 1, 1 - b, i)
                finish(n - 1, 1 - b, i_prev, not known or n >= 3)

            for n in range(1, 4):
                step(n, n % 2, (n + 1) // 2, (n - 1) // 2)
            with pool.Fori(2, NT // 2 - 1) as i:
                step(2 * i, 0, i, i - 1)
                step(2 * i + 1, 1, i + 1, i)
            step(NT - 2, 0, NT // 2 - 1, NT // 2 - 2)
            step(NT - 1, 1, None, NT // 2 - 1)
            finish(NT - 1, 1, NT // 2 - 1)

        @block.vector
        def _(dve):
            v = nc.vector
            count = [0]

            def then(ins):
                count[0] += 1
                ins.then_inc(dve_pre, 1)
                dve.wait_ge(dve_pre, count[0])

            for g in range(NG):
                dve.wait_ge(load_x[g], 16)
                for t in range(g * GT, (g + 1) * GT):
                    v.bn_stats(bn[:, t, :], xs[:, t, :]).then_inc(bn_done, 1)
            dve.wait_ge(bn_done, NT)

            def col(k):
                return bn[:, :, k]

            s_ = [st[:, k, :] for k in range(12)]
            v.tensor_tensor(s_[0], col(1), col(4), ALU.add).then_inc(dve_pre, 1)
            v.tensor_tensor(s_[1], col(1), col(4), ALU.subtract).then_inc(dve_pre, 1)
            count[0] = 2
            then(v.tensor_tensor(s_[2], col(2), col(5), ALU.add))
            then(v.scalar_tensor_tensor(out=s_[3], in0=s_[1], scalar=0.25, in1=s_[1], op0=ALU.mult, op1=ALU.mult))
            then(v.scalar_tensor_tensor(out=s_[3], in0=s_[2], scalar=1.0 / D, in1=s_[3], op0=ALU.mult, op1=ALU.add))
            then(v.tensor_scalar(s_[4], s_[3], LN_EPS, None, ALU.add))
            dve.wait_ge(std_done, 1)
            then(v.reciprocal(s_[6], s_[5]))
            then(v.tensor_tensor(s_[7], s_[6], s_[6], ALU.mult))
            then(v.tensor_tensor(s_[7], s_[7], s_[3], ALU.mult))
            then(v.tensor_scalar(s_[8], s_[7], RMS_EPS, None, ALU.add))
            then(v.tensor_scalar(s_[0], s_[0], 0.5, None, ALU.mult))
            dve.wait_ge(rms_done, 1)
            then(v.reciprocal(s_[10], s_[9]))
            then(v.tensor_tensor(s_[11], s_[6], s_[10], ALU.mult))
            with dve.Fori(0, NG) as i:
                for k in range(GT):
                    t = GT * i + k
                    at = bass.ds(t, 1)
                    v.tensor_scalar(xq[:, at, :], xs[:, at, :], st[:, 0, at], st[:, 11, at], ALU.subtract, ALU.mult)\
                        .then_inc(xq_done, 1)
            dve.wait_ge(load_cst, 16)
            dve.wait_ge(load_w, 16)
            v.tensor_scalar(w_s[:, 0:WG], w_raw[:, 0:WG], c("norm_w"), None, ALU.mult).then_inc(w_scaled, 1)
            v.tensor_copy(w_s[:, WG:WG + E], w_raw[:, WG:WG + E]).then_inc(w_scaled, 1)
            v.tensor_tensor(upto_before[:], c("upto"), c("ident"), ALU.subtract).then_inc(bf_ready, 1)

            dve.wait_ge(small_ps, 1)
            small = bank[2][:, 0:NT * NSM].rearrange("p (t k) -> p t k", k=NSM)
            q = [sm[:, k, :] for k in range(12)]
            q3 = [sm[:, k, :].rearrange("p (t h) -> p t h", h=NH) for k in range(12)]
            then(v.tensor_tensor(q3[0], small[:, :, 0:NH], bc(c("dt_bias").unsqueeze(1), [P, NT, NH]), ALU.add))
            v.scalar_tensor_tensor(out=q[1], in0=q[0], scalar=-1.0, in1=q[0], op0=ALU.mult, op1=ALU.max).then_inc(abs_done, 1)
            R = [r[:, k, :].rearrange("p (t e) -> p t e", e=E) for k in range(10)]
            then(v.tensor_tensor(R[0], small[:, :, NH:NSM], bc(st[:, 9, :].unsqueeze(2), [P, NT, E]), ALU.mult))
            then(v.tensor_tensor(R[1], R[0], bc(c("bg").unsqueeze(1), [P, NT, E]), ALU.add))
            dve.wait_ge(e_done, 1)
            then(v.tensor_scalar(q[3], q[2], 2.0, None, ALU.add))
            then(v.reciprocal(q[4], q[3]))
            then(v.tensor_tensor(q[4], q[4], q[2], ALU.mult))
            then(v.tensor_tensor(q[5], q[4], q[4], ALU.mult))
            then(v.tensor_scalar(q[6], q[5], 1.0 / 15, None, ALU.mult))
            for k in (13, 11, 9, 7, 5, 3):
                then(v.scalar_tensor_tensor(out=q[6], in0=q[6], scalar=1.0 / k, in1=q[5], op0=ALU.add, op1=ALU.mult))
            then(v.scalar_tensor_tensor(out=q[6], in0=q[6], scalar=1.0, in1=q[4], op0=ALU.add, op1=ALU.mult))
            then(v.tensor_scalar(q[7], q[0], 0.0, 0.5, ALU.max, ALU.mult))
            then(v.tensor_tensor(q[7], q[7], q[6], ALU.add))
            dt = pack[:, :, S_DT:S_DT + NH]
            then(v.tensor_scalar(dt, q3[7], 2.0, None, ALU.mult))
            dve.wait_ge(a_exp, 1)
            v.scalar_tensor_tensor(out=decay[:].rearrange("p (t h) -> p t h", h=NH), in0=dt, scalar=-1.0,
                                   in1=bc(neg_a[:].unsqueeze(1), [P, NT, NH]), op0=ALU.mult, op1=ALU.mult)\
                .then_inc(log_decay_done, 1)

            then(v.tensor_reduce(r[:, 2, 0:NT], R[1], AX.X, ALU.max))
            then(v.tensor_tensor(R[3], R[1], bc(r[:, 2, 0:NT].unsqueeze(2), [P, NT, E]), ALU.is_equal))
            first = bc(c("first").unsqueeze(1), [P, NT, E])
            then(v.tensor_tensor(R[3], R[3], first, ALU.mult))
            then(v.tensor_reduce(r[:, 2, 0:NT], R[3], AX.X, ALU.max))
            v.tensor_tensor(hot[:], first, bc(r[:, 2, 0:NT].unsqueeze(2), [P, NT, E]), ALU.is_equal).then_inc(hot_done, 1)
            dve.wait_ge(cum_exp, 1)
            v.tensor_copy(pack[:, :, S_CUM:S_CUM + NH], q3[8])
            v.tensor_tensor(pack[:, :, S_SUF:S_SUF + NH], q3[9], dt, ALU.mult)
            then(v.tensor_copy(pack[:, :, S_TOT:S_TOT + NH], q3[10]))
            dve.wait_ge(rank_ps, 1)
            by_e = [r[:, k, :].rearrange("p (e t) -> p e t", e=E) for k in range(10)]
            then(v.tensor_copy(by_e[4], bank[4][:, NT * E:2 * NT * E].rearrange("p (t e) -> p e t", e=E)))
            then(v.tensor_tensor_scan(r[:, 5, :], c("keep"), r[:, 4, :], 0.0, ALU.mult, ALU.add))
            then(v.tensor_tensor(r[:, 6, :], r[:, 5, :], r[:, 4, :], ALU.subtract))
            total = by_e[5][:, :, NT - 1:NT]
            then(v.tensor_tensor(tiles_cmp[:], bc(total, [P, E, NT]), bc(c("steps").unsqueeze(1), [P, E, NT]), ALU.is_gt))
            then(v.tensor_reduce(n_e[:, 0, :], tiles_cmp[:], AX.X, ALU.add))
            then(v.tensor_tensor_scan(n_e[:, 1, :], c("ones")[:, 0:E], n_e[:, 0, :], 0.0, ALU.mult, ALU.add))
            then(v.tensor_tensor(n_e[:, 2, :], n_e[:, 1, :], n_e[:, 0, :], ALU.subtract))
            then(v.tensor_tensor(te_cmp[:], bc(n_e[:, 1, :].unsqueeze(1), [P, NJ, E]),
                                 bc(c("slot_tile").unsqueeze(2), [P, NJ, E]), ALU.is_le))
            then(v.tensor_reduce(te_f[:], te_cmp[:], AX.X, ALU.add))
            v.tensor_scalar(te[:], te_f[:], float(E - 1), None, ALU.min).then_inc(te_done, 1)
            then(v.tensor_tensor(R[7], bank[4][:, 0:NT * E].rearrange("p (t e) -> p t e", e=E),
                                 by_e[6].rearrange("p e t -> p t e"), ALU.add))
            then(v.scalar_tensor_tensor(out=R[7], in0=bc(n_e[:, 2, :].unsqueeze(1), [P, NT, E]), scalar=float(P),
                                        in1=R[7], op0=ALU.mult, op1=ALU.add))
            then(v.tensor_tensor(R[7], R[7], hot[:], ALU.mult))
            then(v.tensor_reduce(slot_f[:], R[7], AX.X, ALU.add))
            then(v.tensor_copy(slot_i[:, 0, :], slot_f[:]))
            then(v.tensor_scalar(slot_i[:, 1, :], slot_i[:, 0, :], 7, None, ALU.logical_shift_right))
            then(v.tensor_scalar(slot_i[:, 2, :], slot_i[:, 0, :], P - 1, None, ALU.bitwise_and))
            then(v.tensor_copy(slot_hl[:], slot_i[:, 1:3, :]))
            v.tensor_copy(pack[:, :, S_SLOT:S_SLOT + 1].bitcast(I32), slot_i[:, 0, :].unsqueeze(2)).then_inc(pack_done, 1)
            v.tensor_tensor(hot_lo[:], bc(c("iota").unsqueeze(1), [P, NT, P]), bc(slot_hl[:, 1, :].unsqueeze(2), [P, NT, P]),
                            ALU.is_equal)
            then(v.tensor_tensor(hot_hi[:], bc(c("slot_tile").unsqueeze(1), [P, NT, NJ]),
                                 bc(slot_hl[:, 0, :].unsqueeze(2), [P, NT, NJ]), ALU.is_equal))
            then(v.tensor_tensor(tok_hi[:, :, 0, :], hot_hi[:], bc(c("tile_no").unsqueeze(2), [P, NT, NJ]), ALU.mult))
            v.tensor_scalar(tok_hi[:, :, 1, :], hot_hi[:], c("row_no"), None, ALU.mult).then_inc(inv_in, 1)
            dve.wait_ge(inv_ps, 1)
            then(v.tensor_copy(tok_f[:].rearrange("p a j -> p (a j)"), bank[5][:, 0:2 * NJ]))
            v.scalar_tensor_tensor(out=tok_i[:], in0=tok_f[:, 0, :], scalar=float(P), in1=tok_f[:, 1, :],
                                   op0=ALU.mult, op1=ALU.add).then_inc(tok_done, 1)

            def gathered_tile(j, k):
                dve.wait_ge(xgT_ps, j + 1)
                v.tensor_copy(xgT[:, k, :], bank[3][:, 0:P]).then_inc(xgT_done, 1)

            def output_tile(j, k, i=None):
                dve.wait_ge(f_ps, j + 1)
                if i is not None:
                    dve.wait_ge(f_stored[k], 16 * i)
                v.tensor_copy(f_t[:, k, :], bank[6 + k % 2][:, 0:D]).then_inc(f_done, 1)

            cw = c("conv_w")

            def conv_tap(i, h, step):
                k = K - 1 - step
                src = x_raw[:, h, bass.ds((i - 1) * GP + k, GP)]
                w = cw[:, h * K + k:h * K + k + 1]
                if step == 0:
                    dve.wait_ge(raw_done, 2 * i + h - 1)
                    v.tensor_scalar(cv_acc[:, h, 0, :], src, w, c("conv_b")[:, h:h + 1], ALU.mult, ALU.add)\
                        .then_inc(tap, 1)
                    return
                dve.wait_ge(tap, TAPS.index((h, step - 1)) + 1 + 2 * K * (i - 1))
                dst = cv[:, h, bass.ds((i - 1) * GP, GP)] if step == K - 1 else cv_acc[:, h, step % 2, :]
                v.scalar_tensor_tensor(out=dst, in0=src, scalar=w, in1=cv_acc[:, h, (step - 1) % 2, :],
                                       op0=ALU.mult, op1=ALU.add).then_inc(tap, 1)

            AT_TILE = [[], [(0, 0), (0, 1)], [(1, 0), (0, 2), (1, 1)], [(0, 3), (1, 2), (1, 3)]]
            TAPS = sum(AT_TILE, [])

            gathered_tile(0, 0)
            gathered_tile(1, 1)
            for j in range(4):
                gathered_tile(j + 2, (j + 2) % 4)
                output_tile(j, j)
            dve.wait_ge(halo_zero, 1)
            with dve.Fori(1, NG + 1) as i:
                for k in range(4):
                    gathered_tile(4 * i + k + 2, (k + 2) % 4)
                    output_tile(4 * i + k, k, i)
                    for h, tap_step in AT_TILE[k]:
                        conv_tap(i, h, tap_step)
            for j in range(4 * (NG + 1), NJ):
                if j + 2 < NJ:
                    gathered_tile(j + 2, (j + 2) % 4)
                output_tile(j, j % 4, j // 4)

            def chunk_scalars(n, at):
                return bc(pack[:, bass.ds(n, 1), at:at + NH].rearrange("p a h -> p (a h)").unsqueeze(2), [P, NH, HD])

            def next_state(n, b, i, first=False):
                if first:
                    dve.wait_ge(state_zero, 1)
                else:
                    dve.wait_ge(state_done, n)
                v.tensor_tensor(heads(state_d[:, b, :]), heads(state[:, b, :]),
                                chunk_scalars(n, S_TOT), ALU.mult).then_inc(dec_done, 1)
                dve.wait_ge(dec_done, n + 1)
                dve.wait_ge(s_ps, n + 1)
                v.tensor_tensor(state[:, 1 - b, :], state_d[:, b, :], bank[5][:, 0:DI], ALU.add).then_inc(state_done, 1)

            def heads(ap):
                return ap.rearrange("p (h d) -> p h d", h=NH)

            def gated_output(n, b, i, first=False):
                dve.wait_ge(y_ps, n + 1)
                v.tensor_tensor(heads(y[:, 0, :]), heads(bank[4][:, DI:2 * DI]),
                                chunk_scalars(n, S_CUM), ALU.mult).then_inc(y_step, 1)
                dve.wait_ge(xd_done, n + 1)
                v.tensor_tensor(y[:, 1, :], bank[4][:, 0:DI], x_d[:, b, :], ALU.add).then_inc(y_step, 1)
                dve.wait_ge(y_step, 3 * n + 2)
                v.tensor_tensor(y[:, 2, :], y[:, 0, :], y[:, 1, :], ALU.add).then_inc(y_step, 1)
                dve.wait_ge(y_step, 3 * n + 3)
                dve.wait_ge(z_done, n + 1)
                v.tensor_tensor(y_o[:, b, :], y[:, 2, :], z_s[:, b, :], ALU.mult).then_inc(y_done, 1)

            def decayed_scores(n, b):
                dve.wait_ge(g_ps, n + 1)
                v.tensor_tensor(g_m[:, b, :], bank[0][:, 0:P], c("upto"), ALU.mult).then_inc(gm_done, 1)
                dve.wait_ge(gm_done, n + 1)
                v.tensor_tensor(m[:, b, :, :], L[:, bass.ds(n * NH, NH), :], bc(g_m[:, b, :].unsqueeze(1), [P, NH, P]),
                                ALU.mult).then_inc(m_done, 1)

            def block_output(n, b, wait=True):
                dve.wait_ge(o_ps, n + 1)
                v.tensor_tensor(s_c[:, b, :], bank[7][:, 0:D], xn[:, bass.ds(n, 1), :].rearrange("p a d -> p (a d)"),
                                ALU.add).then_inc(s_done, 1)
                dve.wait_ge(s_done, n + 1)
                dve.wait_ge(gc_done, n + 1)
                if wait:
                    dve.wait_ge(oc_done, n - 1)
                v.tensor_tensor(sg_c[:, b, :], s_c[:, b, :], g_c[:, b, :], ALU.mult).then_inc(sg_done, 1)

            dve.wait_ge(L_done, NT)
            decayed_scores(0, 0)

            def step(n, b, i):
                known = isinstance(n, int)
                if not known or n + 1 < NT:
                    decayed_scores(n + 1, 1 - b)
                if not known or n >= 2:
                    dve.wait_ge(yT_ps, n - 1)
                gated_output(n, b, i)
                if not known or n + 1 < NT:
                    next_state(n, b, i, known and n == 0)
                if not known or n >= 1:
                    block_output(n - 1, 1 - b, not known or n >= 3)

            for n in range(4):
                step(n, n % 2, n // 2)
            with dve.Fori(2, NT // 2 - 1) as i:
                step(2 * i, 0, i)
                step(2 * i + 1, 1, i)
            step(NT - 2, 0, NT // 2 - 1)
            step(NT - 1, 1, NT // 2 - 1)
            block_output(NT - 1, 1)


def _lay_out(np, a):
    k = np.arange(P)
    part = {
        "ident": np.eye(P), "upto": k[:, None] <= k[None, :], "after": k[:, None] > k[None, :],
        "ones": np.ones((P, P)), "iota": np.broadcast_to(k, (P, P)),
        "first": np.broadcast_to(E - np.arange(E), (P, E)), "steps": np.broadcast_to(P * np.arange(NT), (P, NT)),
        "tile_no": np.broadcast_to(np.arange(NT), (P, NT)), "row_no": k[:, None],
        "slot_tile": np.broadcast_to(np.arange(NJ), (P, NJ)),
        "keep": np.broadcast_to(np.arange(NT * E) % NT != 0, (P, NT * E)),
    }
    part = {n: p.astype(np.float32) for n, p in part.items()}
    part["norm_w"] = a["L0_attn_norm_w"][:, None]
    part["conv_b"] = a["L0_attn_conv_b"].reshape(2, P).T
    part["conv_w"] = a["L0_attn_conv_w"].reshape(2, P, K).transpose(1, 0, 2).reshape(P, 2 * K)
    for name, key in (("dt_bias", "L0_attn_dt_bias"), ("A_log", "L0_attn_A_log"), ("D", "L0_attn_D"), ("bg", "L0_ffn_bg")):
        part[name] = np.broadcast_to(a[key], (P, a[key].shape[0]))
    return np.concatenate([part[n] for n in _AT], axis=1)


def kernel(**inputs):
    import numpy as np
    import concourse.bacc as bacc
    from concourse.bass_utils import run_bass_kernel_spmd

    a = {k: np.asarray(v) for k, v in inputs.items()}
    w = a["L0_attn_in_proj_w"].T
    z, xx, bb, cc, dt = (w[:, 0:DI], w[:, DI:2 * DI], w[:, 2 * DI:2 * DI + NS], w[:, 2 * DI + NS:2 * DI + 2 * NS],
                         w[:, 2 * DI + 2 * NS:])
    arrays = {
        "x": a["L0_attn_x"],
        "w_in": np.concatenate([z, bb, cc, xx, dt, a["L0_ffn_Wg"]], axis=1),
        "w_out": a["L0_attn_out_proj_w"].T.reshape(2, P, D).transpose(1, 0, 2).reshape(P, 2 * D),
        "w1": a["L0_ffn_W1"],
        "w2": a["L0_ffn_W2"].reshape(E, HC, P, D).transpose(2, 0, 1, 3).reshape(P, E * HC * D),
        "consts": _lay_out(np, a),
    }
    arrays = {k: np.ascontiguousarray(v) for k, v in arrays.items()}
    nc = bacc.Bacc("TRN2", target_bir_lowering=False, num_devices=1)
    aps = {k: nc.dram_tensor(k, v.shape, mybir.dt.from_np(v.dtype), kind="ExternalInput").ap() for k, v in arrays.items()}
    out = nc.dram_tensor("out", (1, T, D), F32, kind="ExternalOutput").ap()
    mamba_moe(nc, **aps, out=out)
    return run_bass_kernel_spmd(nc, [arrays], core_ids=[0]).results[0]["out"]
```

```python
from contextlib import ExitStack

import concourse.bass as bass
from concourse import mybir

F32 = mybir.dt.float32
BF16 = mybir.dt.bfloat16
I32 = mybir.dt.int32
ALU = mybir.AluOpType
ACT = mybir.ActivationFunctionType
AX = mybir.AxisListType

P = 128
D = 128
NS = 128
DI = 256
NH = 4
HD = DI // NH
K = 4
E = 8
HID = 512
HC = HID // P
T = 2048
NT = T // P
NG = 4
GT = NT // NG
GP = GT * P
CONV_0 = 512
CONV_I = (T - CONV_0) // NG
NJ = NT + E - 1
SPLIT = 3
LAG = 3
WARM = 6
LN_EPS = 1e-5
RMS_EPS = 1e-6

WZ, WB, WC, WX, WDT, WG = 0, DI, DI + NS, DI + 2 * NS, 2 * DI + 2 * NS, 2 * DI + 2 * NS + NH
WCOLS = WG + E
NSM = NH + E

_AT = {}
_n = 0
for _name, _w in (("ident", P), ("upto", P), ("after", P), ("ones", P), ("iota", P), ("norm_w", 1), ("conv_b", 2),
                  ("conv_w", 2 * K), ("dt_bias", NH), ("A_log", NH), ("D", NH), ("bg", E), ("first", E),
                  ("steps", NT), ("tile_no", NT), ("row_no", 1), ("slot_tile", NJ), ("keep", NT * E)):
    _AT[_name] = (_n, _w)
    _n += _w
CCOLS = _n
S_DT, S_CUM, S_SUF, S_TOT, SCOLS = 0, 4, 8, 12, 16


def mamba_moe(nc, x, w_in, w_out, w1, w2, consts, out):
    with ExitStack() as ctx:
        def sb(name, shape, dt=F32):
            return ctx.enter_context(nc.sbuf_tensor(name, shape, dt))

        def sem(name):
            return ctx.enter_context(nc.semaphore(name))

        xn_rows = nc.dram_tensor("xn_rows", [T, D], F32, kind="Internal").ap()
        f_rows = nc.dram_tensor("f_rows", [NJ * P, D], F32, kind="Internal").ap()

        cst = sb("cst", [P, CCOLS])

        def c(name):
            at, w = _AT[name]
            return cst[:, at:at + w]

        w_raw = sb("w_raw", [P, WCOLS])
        w_s = sb("w_s", [P, WCOLS])
        wo = sb("wo", [P, 2, D])
        w2_s = sb("w2_s", [P, E * HC * D])
        early = sb("early", [P, NT, P + SCOLS])
        xqT, pack = early[:, :, 0:P], early[:, :, P:P + SCOLS]
        late = sb("late", [P, NT + LAG, 2 * D + 1])
        xq, xs, slot = late[:, 0:NT, 0:D], late[:, LAG:NT + LAG, D:2 * D], late[:, 0:NT, 2 * D:2 * D + 1]
        xn = sb("xn", [P, NT, D])
        bn = sb("bn", [P, NT, 6])
        zeros = sb("zeros", [P, 4 * P], BF16)
        st = sb("st", [P, 12, NT])
        sm = sb("sm", [P, 12, NT * NH])
        neg_a = sb("neg_a", [P, NH])
        decay = sb("decay", [P, NT * NH])
        L = sb("L", [P, NT * NH, P])
        r = sb("r", [P, 8, NT * E])
        hot = sb("hot", [P, NT, E], BF16)
        upto_before = sb("upto_before", [P, P], BF16)
        ones_bf = sb("ones_bf", [P, P], BF16)
        n_e = sb("n_e", [P, 8, E])
        tiles_cmp = sb("tiles_cmp", [P, E, NT])
        te_cmp = sb("te_cmp", [P, NJ, E])
        te_f = sb("te_f", [P, NJ])
        te = sb("te", [P, NJ], I32)
        slot_f = sb("slot_f", [P, NT])
        slot_i = sb("slot_i", [P, 3, NT], I32)
        slot_hl = sb("slot_hl", [P, 2, NT])
        hot_hi = sb("hot_hi", [P, NT, NJ])
        tok_hi = sb("tok_hi", [P, NT, 2, NJ], BF16)
        tok_f = sb("tok_f", [P, 2, NJ])
        tok_i = sb("tok_i", [P, NJ], I32)
        xg = sb("xg", [P, 4, D])
        w1_t = sb("w1_t", [P, 4, HID])
        xgT = sb("xgT", [P, 4, P])
        hT = sb("hT", [P, 2, HC, P])
        f_t = sb("f_t", [P, 4, D])
        early_c = sb("early_c", [P, 2, P + SCOLS])
        late_c = sb("late_c", [P, 2, 2 * D + 1])
        xqT_c, sc = early_c[:, :, 0:P], early_c[:, :, P:P + SCOLS]
        xq_c, x_c, slot_c = late_c[:, :, 0:D], late_c[:, :, D:2 * D], late_c[:, :, 2 * D:2 * D + 1]
        x_raw = sb("x_raw", [P, 2, T + K - 1])
        cv_acc = sb("cv_acc", [P, 2, 2, GP])
        cv = sb("cv", [P, 2, T])
        hot_lo = cv[:, 0, 0:T // 2].bitcast(BF16).rearrange("p (t k) -> p t k", k=P)
        cv_s = sb("cv_s", [P, 2, 2, P])
        w_bcT = sb("w_bcT", [P, 2, D])
        w_bc = sb("w_bc", [P, D])
        vT = sb("vT", [P, 2, P])
        z_s = sb("z_s", [P, 2, DI])
        x_v = sb("x_v", [P, 2, DI])
        m = sb("m", [P, 2, NH, P])
        x_dt = sb("x_dt", [P, 2, DI])
        x_w = sb("x_w", [P, 2, DI])
        x_d = sb("x_d", [P, 2, DI])
        state = sb("state", [P, 2, DI])
        state_d = sb("state_d", [P, 2, DI])
        y = sb("y", [P, 3, DI])
        y_o = sb("y_o", [P, 2, DI])
        yT = sb("yT", [P, 2, 2, P])
        f_c = sb("f_c", [P, 2, D])
        g_c = sb("g_c", [P, 2, D])
        s_c = sb("s_c", [P, 2, D])
        sg_c = sb("sg_c", [P, 2, D])
        o_c = sb("o_c", [P, 2, D])

        bank = [ctx.enter_context(nc.psum_tensor(f"bank{i}", [P, 512], F32)) for i in range(8)]

        load_cst, load_w, load_wo, load_w2 = sem("load_cst"), sem("load_w"), sem("load_wo"), sem("load_w2")
        load_x = [sem(f"load_x{g}") for g in range(NG)]
        xn_stored = sem("xn_stored")
        var_done, mean_done, stats_done, tok_f_done = (sem(n) for n in ("var_done", "mean_done", "stats_done", "tok_f_done"))
        soft_step, route_step = sem("soft_step"), sem("route_step")
        dve_pre = sem("dve_pre")
        bn_done = sem("bn_done")
        std_done, rms_done = sem("std_done"), sem("rms_done")
        w_scaled = sem("w_scaled")
        x_centred, xn_done, xq_done = sem("x_centred"), sem("xn_done"), sem("xq_done")
        xqT_ps, xqT_done = sem("xqT_ps"), sem("xqT_done")
        small_ps = sem("small_ps")
        a_exp, abs_done, e_done, log_decay_done = sem("a_exp"), sem("abs_done"), sem("e_done"), sem("log_decay_done")
        cum_ps, cum_exp, pack_done = sem("cum_ps"), sem("cum_exp"), sem("pack_done")
        spread, seg_ps, L_done, causal = (sem(n) for n in ("spread", "seg_ps", "L_done", "causal"))
        bf_ready, hot_done, rank_ps, te_done, slot_done, inv_in, inv_ps, tok_done = (
            sem(n) for n in ("bf_ready", "hot_done", "rank_ps", "te_done", "slot_done", "inv_in", "inv_ps", "tok_done"))
        gathered = [sem(f"gathered{i}") for i in range(4)]
        w1_loaded = [sem(f"w1_loaded{i}") for i in range(4)]
        f_stored = [sem(f"f_stored{i}") for i in range(4)]
        xgT_ps, xgT_done, h_ps, h_done, f_ps, f_done = (
            sem(n) for n in ("xgT_ps", "xgT_done", "h_ps", "h_done", "f_ps", "f_done"))
        halo_zero, state_zero, warm_zero, ends_zero = (
            sem(n) for n in ("halo_zero", "state_zero", "warm_zero", "ends_zero"))
        early_in = [sem(f"early_in{b}") for b in range(2)]
        late_in = [sem(f"late_in{b}") for b in range(2)]
        w_bcT_ps, w_bcT_done, w_bc_ps, w_bc_done = (sem(n) for n in ("w_bcT_ps", "w_bcT_done", "w_bc_ps", "w_bc_done"))
        f_in = [sem(f"f_in{b}") for b in range(2)]
        out_stored = [sem(f"out_stored{b}") for b in range(2)]
        (x_ps, v_ps, z_ps, y_ps, s_ps, yT_ps, o_ps, g_ps, xvT_ps) = (
            sem(n) for n in ("x_ps", "v_ps", "z_ps", "y_ps", "s_ps", "yT_ps", "o_ps", "g_ps", "xvT_ps"))
        (v_done, z_done, cvs_done, xv_done, yT_done, gc_done) = (
            sem(n) for n in ("v_done", "z_done", "cvs_done", "xv_done", "yT_done", "gc_done"))
        (raw_done, halo_done, tap, state_done, y_step, y_done, m_done, s_done) = (
            sem(n) for n in ("raw_done", "halo_done", "tap", "state_done", "y_step", "y_done", "m_done",
                             "s_done"))
        (xdt_done, xw_done, xd_done, dec_done, sg_done, oc_done) = (
            sem(n) for n in ("xdt_done", "xw_done", "xd_done", "dec_done", "sg_done", "oc_done"))

        x_tiles = x[0].rearrange("(t p) d -> p t d", p=P)
        out_rows = out[0]

        def bc(ap, shape):
            return ap.to_broadcast(shape)

        block = ctx.enter_context(nc.Block())

        @block.sync
        def _(sp):
            for g in range(NG):
                sp.dma_start(xs[:, g * GT:(g + 1) * GT, :], x_tiles[:, g * GT:(g + 1) * GT, :]).then_inc(load_x[g], 16)
            sp.dma_start(cst[:], consts).then_inc(load_cst, 16)
            sp.dma_start(w_raw[:], w_in).then_inc(load_w, 16)
            sp.dma_start(w2_s[:], w2).then_inc(load_w2, 16)
            sp.wait_ge(xn_done, NG)
            sp.dma_start(xn_rows.rearrange("(t p) d -> p t d", p=P), xn[:]).then_inc(xn_stored, 16)
            sp.dma_start(wo[:].rearrange("p c d -> p (c d)"), w_out).then_inc(load_wo, 16)

            def load_w1(j, k):
                e = sp.value_load(te[0:1, bass.ds(j, 1)], min_val=0, max_val=E - 1)
                sp.dma_start(w1_t[:, k, :], w1[bass.ds(e, 1), :, :].rearrange("e p n -> p (e n)")).then_inc(w1_loaded[k], 16)

            def store_f(j, k):
                sp.wait_ge(f_done, j + 1)
                sp.dma_start(f_rows[bass.ds(j * P, P), :], f_t[:, k, :]).then_inc(f_stored[k], 16)

            sp.wait_ge(te_done, 1)
            for k in range(4):
                load_w1(k, k)
            def load_early(n, b):
                sp.dma_start(early_c[:, b, :], early[:, bass.ds(n, 1), :].rearrange("p a d -> p (a d)"))\
                    .then_inc(early_in[b], 16)

            def load_late(n, b):
                sp.dma_start(late_c[:, b, :], late[:, bass.ds(n, 1), :].rearrange("p a d -> p (a d)"))\
                    .then_inc(late_in[b], 16)

            sp.wait_ge(pack_done, 4)
            sp.wait_ge(ends_zero, 3)
            for n in range(2):
                load_early(n, n)
                load_late(n, n)
            with sp.Fori(0, (NJ - 3) // 4 - 1) as i:
                for k in range(4):
                    sp.wait_ge(h_ps, 4 * i + k + 1)
                    load_w1(4 * i + k + 4, k)
                    store_f(4 * i + k, k)
            last = NJ - 7
            for j in range(last, NJ):
                if j + 4 < NJ:
                    sp.wait_ge(h_ps, j + 1)
                    load_w1(j + 4, j % 4)
                store_f(j, j % 4)

            def store_out(n, b):
                sp.wait_ge(oc_done, n + 1)
                sp.dma_start(out_rows[bass.ds(n * P, P), :], o_c[:, b, :]).then_inc(out_stored[b], 16)

            sp.wait_ge(g_ps, 1)
            sp.wait_ge(xdt_done, 1)
            load_early(2, 0)

            def step(n, b, i):
                known = isinstance(n, int)
                if not known or n + 3 < NT:
                    sp.wait_ge(g_ps, n + 2)
                    sp.wait_ge(xdt_done, n + 2)
                    load_early(n + 3, 1 - b)
                if not known or n + 1 < NT:
                    sp.wait_ge(s_ps, n + 1)
                if not known or n < NT:
                    sp.wait_ge(f_in[b], 16 * (i + 1))
                load_late(n + 2, b)
                if not known or n >= 2:
                    store_out(n - 2, b)

            step(0, 0, 0)
            step(1, 1, 0)
            with sp.Fori(1, NT // 2 - 2) as i:
                step(2 * i, 0, i)
                step(2 * i + 1, 1, i)
            for n in range(NT - 4, NT + 1):
                step(n, n % 2, n // 2)
            store_out(NT - 1, 1)
            for b in range(2):
                sp.wait_ge(out_stored[b], 16 * NT // 2)

        @block.tensor
        def _(pe):
            mm, tr = nc.tensor.matmul, nc.tensor.transpose
            ident = c("ident")
            pe.wait_ge(warm_zero, 1)
            with pe.Fori(0, WARM) as i:
                for k in range(4):
                    mm(bank[7][:], zeros[:, 0:P], zeros[:], start=True, stop=True)
            pe.wait_ge(load_cst, 16)

            def transpose_group(g):
                if g >= 2:
                    pe.wait_ge(xqT_done, g - 1)
                for t in range(g * GT, (g + 1) * GT):
                    pe.wait_ge(xq_done, t + 1)
                    ins = tr(bank[g % 2][:, t % GT * P:(t % GT + 1) * P], xq[:, t, :], ident)
                ins.then_inc(xqT_ps, 1)

            def small_products(g):
                pe.wait_ge(xqT_done, g + 1)
                for t in range(g * GT, (g + 1) * GT):
                    ins = mm(bank[2][:, t * NSM:(t + 1) * NSM], xqT[:, t, :], w_s[:, WDT:WDT + NSM],
                             start=True, stop=True)
                return ins

            def conv_channels(g, h, wait=True):
                if wait:
                    pe.wait_ge(raw_done, 2 * g + h - 1)
                mm(bank[6 + h][:].rearrange("p (t k) -> p t k", k=P), w_s[:, WX + h * P:WX + (h + 1) * P], xqT[:, g * GT:(g + 1) * GT, :],
                   start=True, stop=True).then_inc(x_ps, 1)

            transpose_group(0)
            pe.wait_ge(w_scaled, 2)
            for g in range(1, NG):
                transpose_group(g)
                small_products(g - 1)
            small_products(NG - 1).then_inc(small_ps, 1)
            for h, at in enumerate((WB, WC)):
                ins = tr(bank[3][:, h * P:(h + 1) * P], w_s[:, at:at + P], ident)
            ins.then_inc(w_bcT_ps, 1)
            for h in range(2):
                conv_channels(0, h, False)
            pe.wait_ge(w_bcT_done, 1)
            mm(bank[5][:, 0:D], w_bcT[:, 1, :], w_bcT[:, 0, :], start=True, stop=True).then_inc(w_bc_ps, 1)
            conv_channels(1, 0)
            pe.wait_ge(bf_ready, 2)
            pe.wait_ge(hot_done, 1)
            mm(bank[4][:, 0:NT * E], upto_before[:], hot[:].rearrange("p t e -> p (t e)"), start=True, stop=True)
            mm(bank[4][:, NT * E:2 * NT * E], ones_bf[:], hot[:].rearrange("p t e -> p (t e)"), start=True, stop=True)\
                .then_inc(rank_ps, 1)
            conv_channels(1, 1)
            for g in range(2, NG):
                for h in range(2):
                    conv_channels(g, h)
            pe.wait_ge(w_bcT_done, 1)
            pe.wait_ge(log_decay_done, 1)
            for n, mask in enumerate(("upto", "after", "ones")):
                ins = mm(bank[3][:, n * NT * NH:(n + 1) * NT * NH], c(mask), decay[:], start=True, stop=True)
            ins.then_inc(cum_ps, 1)
            pe.wait_ge(xqT_done, NG)

            def log_decays(n, b, wait=True):
                if wait:
                    pe.wait_ge(L_done, n - 1)
                mm(bank[b][:], c("after"), L[:, bass.ds(n * NH, NH), :], start=True, stop=True).then_inc(seg_ps, 1)

            for n in range(2):
                pe.wait_ge(spread, 1)
                log_decays(n, n, False)
            with pe.Fori(1, SPLIT) as i:
                pe.wait_ge(spread, i + 1)
                for b in range(2):
                    log_decays(2 * i + b, b)
            pe.wait_ge(inv_in, 3)
            pe.wait_ge(w_bc_done, 1)
            for t in range(NT):
                ins = mm(bank[5][:, 0:2 * NJ], hot_lo[:, t, :], tok_hi[:, t, :, :].rearrange("p a j -> p (a j)"),
                         start=(t == 0), stop=(t == NT - 1))
            ins.then_inc(inv_ps, 1)
            with pe.Fori(SPLIT, NT // 2) as i:
                pe.wait_ge(spread, i + 1)
                for b in range(2):
                    log_decays(2 * i + b, b)

            def transpose_in(j, k, i, bank_free=True):
                pe.wait_ge(gathered[k], 16 * (i + 1))
                if bank_free:
                    pe.wait_ge(xgT_done, j)
                tr(bank[3][:, 0:P], xg[:, k, :], ident).then_inc(xgT_ps, 1)

            def hidden(j, k, i, bank_free=True):
                pe.wait_ge(w1_loaded[k], 16 * (i + 1))
                pe.wait_ge(xgT_done, j + 1)
                if bank_free:
                    pe.wait_ge(h_done, j - 1)
                for h in range(HC):
                    ins = mm(bank[k % 2][:, h * P:(h + 1) * P], w1_t[:, k, h * P:(h + 1) * P], xgT[:, k, :],
                             start=True, stop=True)
                ins.then_inc(h_ps, 1)

            def back(j, k, bank_free=True):
                e = pe.value_load(te[0:1, bass.ds(j, 1)], min_val=0, max_val=E - 1)
                pe.wait_ge(h_done, j + 1)
                if bank_free:
                    pe.wait_ge(f_done, j - 1)
                for h in range(HC):
                    ins = mm(bank[6 + k % 2][:, 0:D], hT[:, k % 2, h, :], w2_s[:, bass.ds(e * (HC * D) + h * D, D)],
                             start=(h == 0), stop=(h == HC - 1))
                ins.then_inc(f_ps, 1)

            def tile(j, k, i):
                if not isinstance(j, int) or j + 2 < NJ:
                    transpose_in(j + 2, (k + 2) % 4, i + (k + 2) // 4)
                if not isinstance(j, int) or j + 1 < NJ:
                    hidden(j + 1, (k + 1) % 4, i + (k + 1) // 4, not isinstance(j, int) or j >= 1)
                back(j, k, not isinstance(j, int) or j >= 2)

            pe.wait_ge(te_done, 1)
            pe.wait_ge(L_done, NT)
            pe.wait_ge(cum_exp, 1)
            pe.wait_ge(raw_done, 2 * NG)
            transpose_in(0, 0, 0, False)
            transpose_in(1, 1, 0)
            hidden(0, 0, 0, False)
            pe.wait_ge(load_w2, 16)
            for j in range(4):
                tile(j, j, 0)
            with pe.Fori(1, NG + 1) as i:
                for k in range(4):
                    tile(4 * i + k, k, i)
            def project_v(n, b, i, first=False):
                pe.wait_ge(early_in[b], 16 * (i + 1))
                if not first:
                    pe.wait_ge(v_done, n)
                mm(bank[4 if first else 1][:, 0:P], w_bc[:], xqT_c[:, b, :], start=True, stop=True).then_inc(v_ps, 1)

            def project_z(n, b, first=False):
                if not first:
                    pe.wait_ge(z_done, n)
                mm(bank[2][:, 0:DI], xqT_c[:, b, :], w_s[:, WZ:WZ + DI], start=True, stop=True).then_inc(z_ps, 1)

            def transpose_y(n, b, first=False):
                pe.wait_ge(y_done, n + 1)
                if first:
                    pe.wait_ge(f_done, NJ)
                if not first:
                    pe.wait_ge(yT_done, n)
                for h in range(2):
                    ins = tr(bank[6][:, h * P:(h + 1) * P], y_o[:, b, h * P:(h + 1) * P], ident)
                ins.then_inc(yT_ps, 1)

            def chunk_state(n, b, i, first=False):
                pe.wait_ge(xw_done, n + 1)
                pe.wait_ge(late_in[b], 16 * (i + 1))
                if not first:
                    pe.wait_ge(state_done, n)
                mm(bank[5][:, 0:DI], xq_c[:, b, :], x_w[:, b, :], start=True, stop=True).then_inc(s_ps, 1)

            def chunk_output(n, b, first=False):
                if first:
                    pe.wait_ge(state_zero, 1)
                    pe.wait_ge(v_done, 1)
                else:
                    pe.wait_ge(y_step, 3 * n)
                    pe.wait_ge(state_done, n)
                mm(bank[4][:, DI:2 * DI], vT[:, b, :], state[:, b, :], start=True, stop=True)
                pe.wait_ge(m_done, n + 1)
                pe.wait_ge(xdt_done, n + 1)
                for h in range(NH):
                    ins = mm(bank[4][:, h * HD:(h + 1) * HD], m[:, b, h, :], x_dt[:, b, h * HD:(h + 1) * HD],
                             start=True, stop=True)
                ins.then_inc(y_ps, 1)

            def project_out(n, b, first=False):
                pe.wait_ge(yT_done, n + 1)
                if not first:
                    pe.wait_ge(s_done, n)
                for h in range(2):
                    ins = mm(bank[7][:, 0:D], yT[:, b, h, :], wo[:, h, :], start=(h == 0), stop=(h == 1))
                ins.then_inc(o_ps, 1)

            def scores(n, b, first=False):
                pe.wait_ge(v_done, n + 1)
                if not first:
                    pe.wait_ge(m_done, n)
                mm(bank[0][:, 0:P], xqT_c[:, b, :], vT[:, b, :], start=True, stop=True).then_inc(g_ps, 1)

            def transpose_inputs(n, b, first=False):
                pe.wait_ge(cvs_done, n + 1)
                if not first:
                    pe.wait_ge(xv_done, n)
                for h in range(2):
                    ins = tr(bank[3][:, h * P:(h + 1) * P], cv_s[:, b, h, :], ident)
                ins.then_inc(xvT_ps, 1)

            for j in range(4 * (NG + 1), NJ):
                if j == NJ - 1:
                    project_v(0, 0, 0, True)
                    project_z(0, 0, True)
                tile(j, j % 4, j // 4)
            pe.wait_ge(xgT_done, NJ)
            transpose_inputs(0, 0, True)
            pe.wait_ge(h_done, NJ)
            scores(0, 0, True)
            pe.wait_ge(load_wo, 16)

            def step(n, b, i_next, i):
                known = isinstance(n, int)
                more = not known or n + 1 < NT
                if more:
                    project_v(n + 1, 1 - b, i_next)
                    transpose_inputs(n + 1, 1 - b)
                    project_z(n + 1, 1 - b)
                if not known or n >= 2:
                    project_out(n - 2, b, known and n == 2)
                if more:
                    scores(n + 1, 1 - b)
                    chunk_state(n, b, i, known and n == 0)
                chunk_output(n, b, known and n == 0)
                if not known or n >= 1:
                    transpose_y(n - 1, 1 - b, known and n == 1)

            for n in range(4):
                step(n, n % 2, (n + 1) // 2, n // 2)
            with pe.Fori(2, NT // 2 - 1) as i:
                step(2 * i, 0, i, i)
                step(2 * i + 1, 1, i + 1, i)
            for n in (NT - 2, NT - 1):
                step(n, n % 2, (n + 1) // 2, n // 2)
            project_out(NT - 2, 0)
            transpose_y(NT - 1, 1)
            project_out(NT - 1, 1)

        @block.scalar
        def _(act):
            a = nc.scalar.activation
            act.wait_ge(var_done, 2)
            a(st[:, 4:6, :], st[:, 2:4, :], ACT.Sqrt).then_inc(std_done, 1)
            act.wait_ge(load_cst, 16)
            act.wait_ge(load_w, 16)
            a(w_s[:, 0:WG], w_raw[:, 0:WG], ACT.Copy, scale=c("norm_w")).then_inc(w_scaled, 1)
            a(w_s[:, WG:WG + E], w_raw[:, WG:WG + E], ACT.Copy).then_inc(w_scaled, 1)
            a(neg_a[:], c("A_log"), ACT.Exp).then_inc(a_exp, 1)
            for g in range(NG):
                act.wait_ge(xqT_ps, g + 1)
                a(xqT[:, g * GT:(g + 1) * GT, :], bank[g % 2][:].rearrange("p (t k) -> p t k", k=P), ACT.Copy).then_inc(xqT_done, 1)
            act.wait_ge(abs_done, 1)
            a(sm[:, 2, :], sm[:, 1, :], ACT.Exp, scale=-1.0).then_inc(e_done, 1)
            act.wait_ge(w_bcT_ps, 1)
            a(w_bcT[:].rearrange("p h d -> p (h d)"), bank[3][:, 0:2 * P], ACT.Copy).then_inc(w_bcT_done, 1)
            for g in range(NG):
                if g == 1:
                    act.wait_ge(w_bc_ps, 1)
                    a(w_bc[:], bank[5][:, 0:D], ACT.Copy).then_inc(w_bc_done, 1)
                for h in range(2):
                    act.wait_ge(x_ps, 2 * g + h + 1)
                    a(x_raw[:, h, K - 1 + g * GP:K - 1 + (g + 1) * GP], bank[6 + h][:], ACT.Copy).then_inc(raw_done, 1)
            act.wait_ge(cum_ps, 1)
            a(sm[:, 8:11, :].rearrange("p a b -> p (a b)"), bank[3][:, 0:3 * NT * NH], ACT.Exp).then_inc(cum_exp, 1)
            with act.Fori(0, NT // 2) as i:
                for b in range(2):
                    act.wait_ge(seg_ps, 2 * i + b + 1)
                    a(L[:, bass.ds((2 * i + b) * NH, NH), :], bank[b][:].rearrange("p (h t) -> p h t", h=NH), ACT.Exp)\
                        .then_inc(L_done, 1)

            def hidden(j, k):
                act.wait_ge(h_ps, j + 1)
                a(hT[:, k, :, :], bank[k][:].rearrange("p (h t) -> p h t", h=HC), ACT.Gelu_apprx_tanh).then_inc(h_done, 1)

            hidden(0, 0)
            hidden(1, 1)
            for j in (2, 3):
                act.wait_ge(f_ps, j - 1)
                hidden(j, j % 2)
            with act.Fori(1, NG + 1) as i:
                for k in range(4):
                    act.wait_ge(f_ps, 4 * i + k - 1)
                    hidden(4 * i + k, k % 2)
            for j in range(4 * (NG + 1), NJ):
                act.wait_ge(f_ps, j - 1)
                hidden(j, j % 2)

            def v_to_sbuf(n, b, wait=True, first=False):
                act.wait_ge(v_ps, n + 1)
                if wait:
                    act.wait_ge(y_ps, n - 1)
                a(vT[:, b, :], bank[4 if first else 1][:, 0:P], ACT.Copy).then_inc(v_done, 1)

            def y_to_sbuf(n, b, wait=True):
                act.wait_ge(yT_ps, n + 1)
                if wait:
                    act.wait_ge(o_ps, n - 1)
                a(yT[:, b, :, :], bank[6][:, 0:2 * P].rearrange("p (h t) -> p h t", h=2), ACT.Copy).then_inc(yT_done, 1)

            def gates(n, b, wait=True):
                act.wait_ge(z_ps, n + 1)
                if wait:
                    act.wait_ge(y_done, n - 1)
                a(z_s[:, b, :], bank[2][:, 0:DI], ACT.Silu).then_inc(z_done, 1)

            def convolved(n, b, wait=True):
                if wait:
                    act.wait_ge(xvT_ps, n - 1)
                a(cv_s[:, b, :, :], cv[:, :, bass.ds(n * P, P)], ACT.Silu).then_inc(cvs_done, 1)

            def inputs(n, b, wait=True):
                act.wait_ge(xvT_ps, n + 1)
                if wait:
                    act.wait_ge(xd_done, n - 1)
                a(x_v[:, b, :], bank[3][:, 0:DI], ACT.Copy).then_inc(xv_done, 1)

            def moe_gate(n, b, i, wait=True):
                act.wait_ge(f_in[b], 16 * (i + 1))
                if wait:
                    act.wait_ge(sg_done, n - 1)
                a(g_c[:, b, :], f_c[:, b, :], ACT.Silu).then_inc(gc_done, 1)

            v_to_sbuf(0, 0, False, True)
            act.wait_ge(tap, 2 * K * (NG + 1))
            convolved(0, 0, False)
            inputs(0, 0, False)
            convolved(1, 1, False)
            gates(0, 0, False)

            def step(n, b, i_prev):
                known = isinstance(n, int)
                if not known or n + 1 < NT:
                    v_to_sbuf(n + 1, 1 - b, not known or n >= 1)
                    inputs(n + 1, 1 - b, not known or n >= 1)
                if not known or n + 1 < NT:
                    gates(n + 1, 1 - b, not known or n >= 1)
                if not known or n >= 1:
                    moe_gate(n - 1, 1 - b, i_prev, not known or n >= 3)
                if not known or n + 2 < NT:
                    convolved(n + 2, b)
                if not known or n >= 1:
                    y_to_sbuf(n - 1, 1 - b, not known or n >= 3)

            for n in range(4):
                step(n, n % 2, (n - 1) // 2)
            with act.Fori(2, NT // 2 - 1) as i:
                step(2 * i, 0, i - 1)
                step(2 * i + 1, 1, i)
            step(NT - 2, 0, NT // 2 - 2)
            step(NT - 1, 1, NT // 2 - 1)
            y_to_sbuf(NT - 1, 1)
            moe_gate(NT - 1, 1, NT // 2 - 1)

        @block.gpsimd
        def _(pool):
            g = nc.gpsimd
            g.memset(zeros[:], 0.0).then_inc(warm_zero, 1)
            g.memset(x_raw[:, :, 0:K - 1], 0.0).then_inc(halo_zero, 1)
            g.memset(state[:, 0, :], 0.0).then_inc(state_zero, 1)
            g.memset(late[:, 0:LAG, D:2 * D], 0.0).then_inc(ends_zero, 1)
            g.memset(late[:, NT:NT + LAG, 0:D], 0.0).then_inc(ends_zero, 1)
            g.memset(late[:, NT:NT + LAG, 2 * D:2 * D + 1], 0.0).then_inc(ends_zero, 1)
            pool.wait_ge(load_cst, 16)
            g.tensor_copy(ones_bf[:], c("ones")).then_inc(bf_ready, 1)
            for n in range(NG):
                if n == 0:
                    pool.wait_ge(stats_done, 1)
                at = slice(n * GT, (n + 1) * GT)
                g.tensor_tensor(xn[:, at, :], xs[:, at, :], bc(st[:, 0, at].unsqueeze(2), [P, GT, D]), ALU.subtract)\
                    .then_inc(x_centred, 1)
                pool.wait_ge(x_centred, n + 1)
                g.tensor_tensor(xn[:, at, :], xn[:, at, :], bc(st[:, 6, at].unsqueeze(2), [P, GT, D]), ALU.mult)\
                    .then_inc(xn_done, 1)
            pool.wait_ge(log_decay_done, 1)
            for n in range(NT // 2):
                src = decay[:, 2 * NH * n:2 * NH * (n + 1)].unsqueeze(2)
                g.affine_select(out=L[:, 2 * NH * n:2 * NH * (n + 1), :], in_=bc(src, [P, 2 * NH, P]),
                                pattern=[[0, 2 * NH], [1, P]], base=0, channel_multiplier=-1,
                                compare_op=ALU.is_ge, fill=0.0).then_inc(spread, 1)
            pool.wait_ge(tok_done, 1)
            pool.wait_ge(xn_stored, 16)
            for j in range(NJ):
                if j >= 4:
                    pool.wait_ge(xgT_ps, j - 3)
                g.indirect_dma_start(xg[:, j % 4, :], None, xn_rows, bass.IndirectOffsetOnAxis(tok_i[:, j:j + 1], 0))\
                    .then_inc(gathered[j % 4], 16)
                n = j - 4
                if 0 <= n < NT // 2:
                    pool.wait_ge(L_done, 2 * n + 2)
                    at = slice(2 * NH * n, 2 * NH * (n + 1))
                    g.affine_select(out=L[:, at, :], in_=L[:, at, :], pattern=[[0, 2 * NH], [1, P]], base=0,
                                    channel_multiplier=-1, compare_op=ALU.is_ge, fill=0.0).then_inc(causal, 1)

            def heads(ap):
                return ap.rearrange("p (h d) -> p h d", h=NH)

            def per_head(b, at):
                return bc(sc[:, b, at:at + NH].unsqueeze(2), [P, NH, HD])

            def gather_output(b):
                g.indirect_dma_start(f_c[:, b, :], None, f_rows,
                                     bass.IndirectOffsetOnAxis(slot_c[:, b, :].bitcast(I32), 0)).then_inc(f_in[b], 16)

            def scaled_inputs(n, b, i, first=False):
                pool.wait_ge(xv_done, n + 1)
                pool.wait_ge(early_in[b], 16 * (i + 1))
                if not first:
                    pool.wait_ge(s_ps, n - 1)
                    pool.wait_ge(y_ps, n - 1)
                g.tensor_tensor(heads(x_w[:, b, :]), heads(x_v[:, b, :]), per_head(b, S_SUF), ALU.mult).then_inc(xw_done, 1)
                g.tensor_tensor(heads(x_dt[:, b, :]), heads(x_v[:, b, :]), per_head(b, S_DT), ALU.mult).then_inc(xdt_done, 1)
                if not first:
                    pool.wait_ge(y_done, n - 1)
                g.tensor_tensor(heads(x_d[:, b, :]), heads(x_v[:, b, :]), bc(c("D").unsqueeze(2), [P, NH, HD]),
                                ALU.mult).then_inc(xd_done, 1)

            def finish(n, b, i, wait=True):
                pool.wait_ge(late_in[1 - b], 16 * (i + 2 + b))
                if wait:
                    pool.wait_ge(out_stored[b], 16 * i)
                pool.wait_ge(sg_done, n + 1)
                g.tensor_tensor(o_c[:, b, :], sg_c[:, b, :], x_c[:, 1 - b, :], ALU.add).then_inc(oc_done, 1)

            scaled_inputs(0, 0, 0, True)
            scaled_inputs(1, 1, 0, True)
            for b in range(2):
                pool.wait_ge(late_in[b], 16)
            for k in range(4):
                pool.wait_ge(f_stored[k], 16 * ((NJ - k + 3) // 4))
            for b in range(2):
                gather_output(b)

            def step(n, b, i, i_prev):
                known = isinstance(n, int)
                more = not known or n + 1 < NT
                if more:
                    scaled_inputs(n + 1, 1 - b, i)
                    pool.wait_ge(late_in[1 - b], 16 * (i + 1))
                    pool.wait_ge(gc_done, n)
                if not known or n >= 2:
                    finish(n - 2, b, i_prev, not known or n >= 4)
                if more:
                    gather_output(1 - b)

            for n in range(1, 4):
                step(n, n % 2, (n + 1) // 2, n // 2 - 1)
            with pool.Fori(2, NT // 2 - 1) as i:
                step(2 * i, 0, i, i - 1)
                step(2 * i + 1, 1, i + 1, i - 1)
            step(NT - 2, 0, NT // 2 - 1, NT // 2 - 2)
            step(NT - 1, 1, None, NT // 2 - 2)
            for b in range(2):
                finish(NT - 2 + b, b, NT // 2 - 1)

        @block.vector
        def _(dve):
            v = nc.vector
            count = [0]

            def then(ins):
                count[0] += 1
                ins.then_inc(dve_pre, 1)
                dve.wait_ge(dve_pre, count[0])

            for g in range(NG):
                dve.wait_ge(load_x[g], 16)
                for t in range(g * GT, (g + 1) * GT):
                    v.bn_stats(bn[:, t, :], xs[:, t, :]).then_inc(bn_done, 1)
            dve.wait_ge(bn_done, NT)

            def col(k):
                return bn[:, :, k]

            s_ = [st[:, k, :] for k in range(12)]
            v.tensor_tensor(s_[9], col(1), col(4), ALU.subtract).then_inc(dve_pre, 1)
            v.tensor_tensor(s_[10], col(2), col(5), ALU.add).then_inc(dve_pre, 1)
            v.tensor_tensor(s_[0], col(1), col(4), ALU.add).then_inc(dve_pre, 1)
            count[0] = 3
            dve.wait_ge(dve_pre, 1)
            v.scalar_tensor_tensor(out=s_[11], in0=s_[9], scalar=0.25, in1=s_[9], op0=ALU.mult, op1=ALU.mult)\
                .then_inc(dve_pre, 1)
            count[0] = 4
            dve.wait_ge(dve_pre, 4)
            then(v.scalar_tensor_tensor(out=s_[11], in0=s_[10], scalar=1.0 / D, in1=s_[11], op0=ALU.mult, op1=ALU.add))
            v.tensor_scalar(s_[2], s_[11], LN_EPS, None, ALU.add).then_inc(var_done, 1)
            v.tensor_scalar(s_[3], s_[11], 1.0 + RMS_EPS, RMS_EPS * LN_EPS, ALU.mult, ALU.add).then_inc(var_done, 1)
            v.tensor_scalar(s_[0], s_[0], 0.5, None, ALU.mult).then_inc(mean_done, 1)
            dve.wait_ge(std_done, 1)
            v.reciprocal(st[:, 6:8, :], st[:, 4:6, :]).then_inc(stats_done, 1)
            dve.wait_ge(mean_done, 1)
            dve.wait_ge(stats_done, 1)
            for t in range(NT):
                v.tensor_scalar(xq[:, t, :], xs[:, t, :], st[:, 0, t:t + 1], st[:, 7, t:t + 1], ALU.subtract, ALU.mult)\
                    .then_inc(xq_done, 1)
            v.tensor_tensor(s_[8], s_[5], s_[6], ALU.mult).then_inc(rms_done, 1)
            dve.wait_ge(load_cst, 16)
            v.tensor_tensor(upto_before[:], c("upto"), c("ident"), ALU.subtract).then_inc(bf_ready, 1)

            soft_count, route_count = [0], [0]

            def soft(ins):
                soft_count[0] += 1
                ins.then_inc(soft_step, 1)

            def route(ins):
                route_count[0] += 1
                ins.then_inc(route_step, 1)

            def after_soft():
                dve.wait_ge(soft_step, soft_count[0])

            def after_route():
                dve.wait_ge(route_step, route_count[0])

            small = bank[2][:, 0:NT * NSM].rearrange("p (t k) -> p t k", k=NSM)
            q = [sm[:, k, :] for k in range(12)]
            q3 = [sm[:, k, :].rearrange("p (t h) -> p t h", h=NH) for k in range(12)]
            R = [r[:, k, :].rearrange("p (t e) -> p t e", e=E) for k in range(8)]
            by_e = [r[:, k, :].rearrange("p (e t) -> p e t", e=E) for k in range(8)]
            first = bc(c("first").unsqueeze(1), [P, NT, E])
            dt = pack[:, :, S_DT:S_DT + NH]

            dve.wait_ge(small_ps, 1)
            soft(v.tensor_tensor(q3[0], small[:, :, 0:NH], bc(c("dt_bias").unsqueeze(1), [P, NT, NH]), ALU.add))
            dve.wait_ge(rms_done, 1)
            route(v.tensor_tensor(R[0], small[:, :, NH:NSM], bc(s_[8].unsqueeze(2), [P, NT, E]), ALU.mult))
            after_soft()
            v.scalar_tensor_tensor(out=q[1], in0=q[0], scalar=-1.0, in1=q[0], op0=ALU.mult, op1=ALU.max).then_inc(abs_done, 1)
            after_route()
            route(v.tensor_tensor(R[1], R[0], bc(c("bg").unsqueeze(1), [P, NT, E]), ALU.add))
            soft(v.tensor_scalar(q[7], q[0], 0.0, 0.5, ALU.max, ALU.mult))
            after_route()
            route(v.tensor_reduce(r[:, 2, 0:NT], R[1], AX.X, ALU.max))
            dve.wait_ge(e_done, 1)
            soft(v.tensor_scalar(q[3], q[2], 2.0, None, ALU.add))
            after_route()
            route(v.tensor_tensor(R[3], R[1], bc(r[:, 2, 0:NT].unsqueeze(2), [P, NT, E]), ALU.is_equal))
            after_soft()
            soft(v.reciprocal(q[4], q[3]))
            after_route()
            route(v.tensor_tensor(R[3], R[3], first, ALU.mult))
            after_soft()
            soft(v.tensor_tensor(q[4], q[4], q[2], ALU.mult))
            after_route()
            route(v.tensor_reduce(r[:, 2, 0:NT], R[3], AX.X, ALU.max))
            after_soft()
            soft(v.tensor_tensor(q[5], q[4], q[4], ALU.mult))
            after_route()
            v.tensor_tensor(hot[:], first, bc(r[:, 2, 0:NT].unsqueeze(2), [P, NT, E]), ALU.is_equal).then_inc(hot_done, 1)
            after_soft()
            soft(v.tensor_scalar(q[6], q[5], 1.0 / 15, None, ALU.mult))

            def series(k):
                after_soft()
                soft(v.scalar_tensor_tensor(out=q[6], in0=q[6], scalar=1.0 / k, in1=q[5], op0=ALU.add, op1=ALU.mult))

            for k in (13, 11, 9):
                series(k)
            dve.wait_ge(rank_ps, 1)
            route(v.tensor_copy(by_e[4], bank[4][:, NT * E:2 * NT * E].rearrange("p (t e) -> p e t", e=E)))
            series(7)
            after_route()
            route(v.tensor_tensor_scan(r[:, 5, :], c("keep"), r[:, 4, :], 0.0, ALU.mult, ALU.add))
            series(5)
            after_route()
            route(v.tensor_tensor(r[:, 6, :], r[:, 5, :], r[:, 4, :], ALU.subtract))
            series(3)
            total = by_e[5][:, :, NT - 1:NT]
            route(v.tensor_tensor(tiles_cmp[:], bc(total, [P, E, NT]), bc(c("steps").unsqueeze(1), [P, E, NT]), ALU.is_gt))
            after_soft()
            soft(v.scalar_tensor_tensor(out=q[6], in0=q[6], scalar=1.0, in1=q[4], op0=ALU.add, op1=ALU.mult))
            after_route()
            route(v.tensor_reduce(n_e[:, 0, :], tiles_cmp[:], AX.X, ALU.add))
            after_soft()
            soft(v.tensor_tensor(q[7], q[7], q[6], ALU.add))
            after_route()
            route(v.tensor_tensor_scan(n_e[:, 1, :], c("ones")[:, 0:E], n_e[:, 0, :], 0.0, ALU.mult, ALU.add))
            after_soft()
            soft(v.tensor_scalar(dt, q3[7], 2.0, None, ALU.mult))
            after_soft()
            dve.wait_ge(a_exp, 1)
            v.scalar_tensor_tensor(out=decay[:].rearrange("p (t h) -> p t h", h=NH), in0=dt, scalar=-1.0,
                                   in1=bc(neg_a[:].unsqueeze(1), [P, NT, NH]), op0=ALU.mult, op1=ALU.mult)\
                .then_inc(log_decay_done, 1)
            after_route()
            route(v.tensor_tensor(te_cmp[:], bc(n_e[:, 1, :].unsqueeze(1), [P, NJ, E]),
                                  bc(c("slot_tile").unsqueeze(2), [P, NJ, E]), ALU.is_le))
            route(v.tensor_tensor(n_e[:, 2, :], n_e[:, 1, :], n_e[:, 0, :], ALU.subtract))
            after_route()
            route(v.tensor_tensor(R[7], bank[4][:, 0:NT * E].rearrange("p (t e) -> p t e", e=E),
                                  by_e[6].rearrange("p e t -> p t e"), ALU.add))
            route(v.tensor_reduce(te_f[:], te_cmp[:], AX.X, ALU.add))
            after_route()
            route(v.scalar_tensor_tensor(out=R[7], in0=bc(n_e[:, 2, :].unsqueeze(1), [P, NT, E]), scalar=float(P),
                                         in1=R[7], op0=ALU.mult, op1=ALU.add))
            v.tensor_scalar(te[:], te_f[:], float(E - 1), None, ALU.min).then_inc(te_done, 1)
            after_route()
            route(v.tensor_tensor(R[7], R[7], hot[:], ALU.mult))
            after_route()
            route(v.tensor_reduce(slot_f[:], R[7], AX.X, ALU.add))
            after_route()
            route(v.tensor_copy(slot_i[:, 0, :], slot_f[:]))
            after_route()
            route(v.tensor_scalar(slot_i[:, 1, :], slot_i[:, 0, :], 7, None, ALU.logical_shift_right))
            route(v.tensor_scalar(slot_i[:, 2, :], slot_i[:, 0, :], P - 1, None, ALU.bitwise_and))
            after_route()
            route(v.tensor_copy(slot_hl[:], slot_i[:, 1:3, :]))
            v.tensor_copy(slot.bitcast(I32), slot_i[:, 0, :].unsqueeze(2)).then_inc(pack_done, 1)
            after_route()
            route(v.tensor_tensor(hot_hi[:], bc(c("slot_tile").unsqueeze(1), [P, NT, NJ]),
                                  bc(slot_hl[:, 0, :].unsqueeze(2), [P, NT, NJ]), ALU.is_equal))
            v.tensor_tensor(hot_lo, bc(c("iota").unsqueeze(1), [P, NT, P]), bc(slot_hl[:, 1, :].unsqueeze(2), [P, NT, P]),
                            ALU.is_equal).then_inc(inv_in, 1)
            after_route()
            v.tensor_tensor(tok_hi[:, :, 0, :], hot_hi[:], bc(c("tile_no").unsqueeze(2), [P, NT, NJ]), ALU.mult).then_inc(inv_in, 1)
            v.tensor_scalar(tok_hi[:, :, 1, :], hot_hi[:], c("row_no"), None, ALU.mult).then_inc(inv_in, 1)
            dve.wait_ge(cum_exp, 1)
            v.tensor_copy(pack[:, :, S_CUM:S_CUM + NH], q3[8]).then_inc(pack_done, 1)
            v.tensor_tensor(pack[:, :, S_SUF:S_SUF + NH], q3[9], dt, ALU.mult).then_inc(pack_done, 1)
            v.tensor_copy(pack[:, :, S_TOT:S_TOT + NH], q3[10]).then_inc(pack_done, 1)
            dve.wait_ge(inv_ps, 1)
            v.tensor_copy(tok_f[:].rearrange("p a j -> p (a j)"), bank[5][:, 0:2 * NJ]).then_inc(tok_f_done, 1)
            dve.wait_ge(tok_f_done, 1)
            v.scalar_tensor_tensor(out=tok_i[:], in0=tok_f[:, 0, :], scalar=float(P), in1=tok_f[:, 1, :],
                                   op0=ALU.mult, op1=ALU.add).then_inc(tok_done, 1)

            def gathered_tile(j, k):
                dve.wait_ge(xgT_ps, j + 1)
                v.tensor_copy(xgT[:, k, :], bank[3][:, 0:P]).then_inc(xgT_done, 1)

            def output_tile(j, k, i=None):
                dve.wait_ge(f_ps, j + 1)
                if i is not None:
                    dve.wait_ge(f_stored[k], 16 * i)
                v.tensor_copy(f_t[:, k, :], bank[6 + k % 2][:, 0:D]).then_inc(f_done, 1)

            cw = c("conv_w")

            def conv_tap(i, h, step):
                k = K - 1 - step
                at, size = (0, CONV_0) if i is None else ((i - 1) * CONV_I + CONV_0, CONV_I)
                src = x_raw[:, h, bass.ds(at + k, size)]
                w = cw[:, h * K + k:h * K + k + 1]
                if step == 0:
                    if i is not None:
                        dve.wait_ge(tap, TAPS.index((h, K - 1)) + 1 + 2 * K * (i - 1))
                    v.tensor_scalar(cv_acc[:, h, 0, 0:size], src, w, c("conv_b")[:, h:h + 1], ALU.mult, ALU.add)\
                        .then_inc(tap, 1)
                    return
                done = TAPS.index((h, step - 1)) + 1
                dve.wait_ge(tap, done if i is None else done + 2 * K * i)
                dst = cv[:, h, bass.ds(at, size)] if step == K - 1 else cv_acc[:, h, step % 2, 0:size]
                v.scalar_tensor_tensor(out=dst, in0=src, scalar=w, in1=cv_acc[:, h, (step - 1) % 2, 0:size],
                                       op0=ALU.mult, op1=ALU.add).then_inc(tap, 1)

            AT_TILE = [[(0, 0), (1, 0)], [(0, 1), (1, 1)], [(0, 2), (1, 2)], [(0, 3), (1, 3)]]
            TAPS = sum(AT_TILE, [])

            dve.wait_ge(halo_zero, 1)
            dve.wait_ge(raw_done, 2 * NG)
            for h, tap_step in TAPS:
                conv_tap(None, h, tap_step)
            gathered_tile(0, 0)
            gathered_tile(1, 1)
            for j in range(4):
                gathered_tile(j + 2, (j + 2) % 4)
                output_tile(j, j)
            with dve.Fori(1, NG + 1) as i:
                for k in range(4):
                    gathered_tile(4 * i + k + 2, (k + 2) % 4)
                    output_tile(4 * i + k, k, i)
                    for h, tap_step in AT_TILE[k]:
                        conv_tap(i, h, tap_step)
            for j in range(4 * (NG + 1), NJ):
                if j + 2 < NJ:
                    gathered_tile(j + 2, (j + 2) % 4)
                output_tile(j, j % 4, j // 4)

            def chunk_scalars(n, at):
                return bc(pack[:, bass.ds(n, 1), at:at + NH].rearrange("p a h -> p (a h)").unsqueeze(2), [P, NH, HD])

            def decayed_state(n, b, first=False):
                if first:
                    dve.wait_ge(state_zero, 1)
                else:
                    dve.wait_ge(state_done, n)
                v.tensor_tensor(heads(state_d[:, b, :]), heads(state[:, b, :]),
                                chunk_scalars(n, S_TOT), ALU.mult).then_inc(dec_done, 1)

            def next_state(n, b):
                dve.wait_ge(dec_done, n + 1)
                dve.wait_ge(s_ps, n + 1)
                v.tensor_tensor(state[:, 1 - b, :], state_d[:, b, :], bank[5][:, 0:DI], ALU.add).then_inc(state_done, 1)

            def heads(ap):
                return ap.rearrange("p (h d) -> p h d", h=NH)

            def decayed_scores(n, b):
                dve.wait_ge(g_ps, n + 1)
                v.tensor_tensor(m[:, b, :, :], L[:, bass.ds(n * NH, NH), :], bc(bank[0][:, 0:P].unsqueeze(1), [P, NH, P]),
                                ALU.mult).then_inc(m_done, 1)

            def with_tokens(n, b):
                dve.wait_ge(o_ps, n + 1)
                v.tensor_tensor(s_c[:, b, :], bank[7][:, 0:D], xn[:, bass.ds(n, 1), :].rearrange("p a d -> p (a d)"),
                                ALU.add).then_inc(s_done, 1)

            def times_mixture(n, b, wait=True):
                dve.wait_ge(s_done, n + 1)
                dve.wait_ge(gc_done, n + 1)
                if wait:
                    dve.wait_ge(oc_done, n - 1)
                v.tensor_tensor(sg_c[:, b, :], s_c[:, b, :], g_c[:, b, :], ALU.mult).then_inc(sg_done, 1)

            dve.wait_ge(causal, NT // 2)
            decayed_state(0, 0, True)
            decayed_scores(0, 0)

            def step(n, b):
                known = isinstance(n, int)
                more = not known or n + 1 < NT
                late = not known or n >= 2
                if late:
                    with_tokens(n - 2, b)
                if more:
                    decayed_scores(n + 1, 1 - b)
                if late:
                    times_mixture(n - 2, b, not known or n >= 4)
                if more:
                    next_state(n, b)
                dve.wait_ge(y_ps, n + 1)
                v.tensor_tensor(heads(y[:, 0, :]), heads(bank[4][:, DI:2 * DI]),
                                chunk_scalars(n, S_CUM), ALU.mult).then_inc(y_step, 1)
                dve.wait_ge(xd_done, n + 1)
                v.tensor_tensor(y[:, 1, :], bank[4][:, 0:DI], x_d[:, b, :], ALU.add).then_inc(y_step, 1)
                if not known or n + 2 < NT:
                    decayed_state(n + 1, 1 - b)
                dve.wait_ge(y_step, 3 * n + 2)
                v.tensor_tensor(y[:, 2, :], y[:, 0, :], y[:, 1, :], ALU.add).then_inc(y_step, 1)
                dve.wait_ge(y_step, 3 * n + 3)
                dve.wait_ge(z_done, n + 1)
                if late:
                    dve.wait_ge(yT_ps, n - 1)
                v.tensor_tensor(y_o[:, b, :], y[:, 2, :], z_s[:, b, :], ALU.mult).then_inc(y_done, 1)

            for n in range(4):
                step(n, n % 2)
            with dve.Fori(2, NT // 2 - 1) as i:
                step(2 * i, 0)
                step(2 * i + 1, 1)
            for b in range(2):
                step(NT - 2 + b, b)
            for b in range(2):
                with_tokens(NT - 2 + b, b)
                times_mixture(NT - 2 + b, b)


def _lay_out(np, a):
    k = np.arange(P)
    part = {
        "ident": np.eye(P), "upto": k[:, None] <= k[None, :], "after": k[:, None] > k[None, :],
        "ones": np.ones((P, P)), "iota": np.broadcast_to(k, (P, P)),
        "first": np.broadcast_to(E - np.arange(E), (P, E)), "steps": np.broadcast_to(P * np.arange(NT), (P, NT)),
        "tile_no": np.broadcast_to(np.arange(NT), (P, NT)), "row_no": k[:, None],
        "slot_tile": np.broadcast_to(np.arange(NJ), (P, NJ)),
        "keep": np.broadcast_to(np.arange(NT * E) % NT != 0, (P, NT * E)),
    }
    part = {n: p.astype(np.float32) for n, p in part.items()}
    part["norm_w"] = a["L0_attn_norm_w"][:, None]
    part["conv_b"] = a["L0_attn_conv_b"].reshape(2, P).T
    part["conv_w"] = a["L0_attn_conv_w"].reshape(2, P, K).transpose(1, 0, 2).reshape(P, 2 * K)
    for name, key in (("dt_bias", "L0_attn_dt_bias"), ("A_log", "L0_attn_A_log"), ("D", "L0_attn_D"), ("bg", "L0_ffn_bg")):
        part[name] = np.broadcast_to(a[key], (P, a[key].shape[0]))
    return np.concatenate([part[n] for n in _AT], axis=1)


def kernel(**inputs):
    import numpy as np
    import concourse.bacc as bacc
    from concourse.bass_utils import run_bass_kernel_spmd

    a = {k: np.asarray(v) for k, v in inputs.items()}
    w = a["L0_attn_in_proj_w"].T
    z, xx, bb, cc, dt = (w[:, 0:DI], w[:, DI:2 * DI], w[:, 2 * DI:2 * DI + NS], w[:, 2 * DI + NS:2 * DI + 2 * NS],
                         w[:, 2 * DI + 2 * NS:])
    arrays = {
        "x": a["L0_attn_x"],
        "w_in": np.concatenate([z, bb, cc, xx, dt, a["L0_ffn_Wg"]], axis=1),
        "w_out": a["L0_attn_out_proj_w"].T.reshape(2, P, D).transpose(1, 0, 2).reshape(P, 2 * D),
        "w1": a["L0_ffn_W1"],
        "w2": a["L0_ffn_W2"].reshape(E, HC, P, D).transpose(2, 0, 1, 3).reshape(P, E * HC * D),
        "consts": _lay_out(np, a),
    }
    arrays = {k: np.ascontiguousarray(v) for k, v in arrays.items()}
    nc = bacc.Bacc("TRN2", target_bir_lowering=False, num_devices=1)
    aps = {k: nc.dram_tensor(k, v.shape, mybir.dt.from_np(v.dtype), kind="ExternalInput").ap() for k, v in arrays.items()}
    out = nc.dram_tensor("out", (1, T, D), F32, kind="ExternalOutput").ap()
    mamba_moe(nc, **aps, out=out)
    return run_bass_kernel_spmd(nc, [arrays], core_ids=[0]).results[0]["out"]
```
